# Optimizing a Trainium2 kernel written in Bass

```python
import numpy as np
import jax
import jax.numpy as jnp

def _softmax(x, axis=-1):
    return jax.nn.softmax(x, axis=axis)

def _gelu(x):
    return jax.nn.gelu(x, approximate=True)

def _silu(x):
    return jax.nn.silu(x)

def _sigmoid(x):
    return jax.nn.sigmoid(x)

def _layernorm(x, axis=-1, eps=1e-05):
    m = jnp.mean(x, axis=axis, keepdims=True)
    v = jnp.var(x, axis=axis, keepdims=True)
    return (x - m) / jnp.sqrt(v + eps)

def _scatter_add(tgt, idx, src, axis=0):
    return tgt.at[idx].add(src)

def _segment_sum(src, seg, n):
    return jax.ops.segment_sum(src, seg, n)
kernel_name = 'mk_vit_tower_postln_d1_tok_img768_r4_cf29c6'

def setup_inputs(seed: int=0):
    np.random.seed(seed)
    _w = jnp.asarray

    def _rec_inputs():
        import jax
        import jax.numpy as jnp
        _rk = jax.random.key(seed)
        x = -0.00016672 + 0.999947 * jax.random.normal(jax.random.fold_in(_rk, 1), (64, 3, 64, 64), jnp.float32)
        return x
    x = _rec_inputs()

    def _L0_tok_setup():
        import jax, jax.numpy as jnp
        import numpy as np
        CHANNEL = 3
        PATCH = 16
        D_MODEL = 192
        key = jax.random.key(seed)
        kx, kw = jax.random.split(key)
        x = jax.random.normal(kx, (64, CHANNEL, 96, 96), dtype=jnp.float32)
        fan_in = PATCH * PATCH * CHANNEL
        bound = 1.0 / np.sqrt(fan_in)
        W = jax.random.uniform(kw, (D_MODEL, fan_in), dtype=jnp.float32, minval=-bound, maxval=bound)
        return {'x': x, 'W': W}
    _L0_tok_all = _L0_tok_setup()
    _L0_tok_in = {k: v for k, v in _L0_tok_all.items() if k in ('W',)}
    del _L0_tok_all

    def _L0_attn_setup():
        import jax, jax.numpy as jnp
        import numpy as np
        FEATS = 192
        HEAD = 12
        HD = FEATS // HEAD
        B, N = (128, 197)
        key = jax.random.key(seed)
        k0, k1, k2 = jax.random.split(key, 3)
        x = jax.random.normal(k0, (B, N, FEATS), dtype=jnp.float32)
        W_qkv = jax.random.normal(k1, (HEAD, HD, 3 * HD), dtype=jnp.float32) * 0.05
        b_qkv = jnp.zeros((HEAD, 3 * HD), dtype=jnp.float32)
        W_out = jax.random.normal(k2, (FEATS, FEATS), dtype=jnp.float32) * 0.02
        b_out = jnp.zeros((FEATS,), dtype=jnp.float32)
        return {'x': x, 'W_qkv': W_qkv, 'b_qkv': b_qkv, 'W_out': W_out, 'b_out': b_out}
    _L0_attn_all = _L0_attn_setup()
    _L0_attn_in = {k: v for k, v in _L0_attn_all.items() if k in ('W_qkv', 'b_qkv', 'W_out', 'b_out')}
    del _L0_attn_all

    def _L0_ffn_setup():
        import jax, jax.numpy as jnp
        import numpy as np
        B, N, DIM, HEADS = (4, 256, 192, 12)
        HIDDEN, E, TOPK = (768, 8, 2)
        EPS = 1e-05

        def _layernorm(x, g, b):
            mu = jnp.mean(x, axis=-1, keepdims=True)
            var = jnp.var(x, axis=-1, keepdims=True)
            return (x - mu) * jax.lax.rsqrt(var + EPS) * g + b
        key = jax.random.key(seed)
        ks = jax.random.split(key, 10)
        s = 0.02
        return {'x': jax.random.normal(ks[0], (B, N, DIM), dtype=jnp.float32), 'ln1_g': jnp.ones((DIM,), jnp.float32), 'ln1_b': jnp.zeros((DIM,), jnp.float32), 'qkv_w': jax.random.normal(ks[1], (3 * DIM, DIM), jnp.float32) * s, 'proj_w': jax.random.normal(ks[2], (DIM, DIM), jnp.float32) * s, 'proj_b': jnp.zeros((DIM,), jnp.float32), 'ln2_g': jnp.ones((DIM,), jnp.float32), 'ln2_b': jnp.zeros((DIM,), jnp.float32), 'gate_w': jax.random.normal(ks[3], (E, DIM), jnp.float32) * s, 'gate_b': jnp.zeros((E,), jnp.float32), 'w1': jax.random.normal(ks[4], (E, HIDDEN, DIM), jnp.float32) * s, 'b1': jnp.zeros((E, HIDDEN), jnp.float32), 'w2': jax.random.normal(ks[5], (E, DIM, HIDDEN), jnp.float32) * s, 'b2': jnp.zeros((E, DIM), jnp.float32)}
    _L0_ffn_all = _L0_ffn_setup()
    _L0_ffn_in = {k: v for k, v in _L0_ffn_all.items() if k in ('ln1_g', 'ln1_b', 'qkv_w', 'proj_w', 'proj_b', 'ln2_g', 'ln2_b', 'gate_w', 'gate_b', 'w1', 'b1', 'w2', 'b2')}
    del _L0_ffn_all
    return {'x': x, 'L0_tok_W': _L0_tok_in['W'], 'L0_attn_W_qkv': _L0_attn_in['W_qkv'], 'L0_attn_b_qkv': _L0_attn_in['b_qkv'], 'L0_attn_W_out': _L0_attn_in['W_out'], 'L0_attn_b_out': _L0_attn_in['b_out'], 'L0_ffn_ln1_g': _L0_ffn_in['ln1_g'], 'L0_ffn_ln1_b': _L0_ffn_in['ln1_b'], 'L0_ffn_qkv_w': _L0_ffn_in['qkv_w'], 'L0_ffn_proj_w': _L0_ffn_in['proj_w'], 'L0_ffn_proj_b': _L0_ffn_in['proj_b'], 'L0_ffn_ln2_g': _L0_ffn_in['ln2_g'], 'L0_ffn_ln2_b': _L0_ffn_in['ln2_b'], 'L0_ffn_gate_w': _L0_ffn_in['gate_w'], 'L0_ffn_gate_b': _L0_ffn_in['gate_b'], 'L0_ffn_w1': _L0_ffn_in['w1'], 'L0_ffn_b1': _L0_ffn_in['b1'], 'L0_ffn_w2': _L0_ffn_in['w2'], 'L0_ffn_b2': _L0_ffn_in['b2']}

def reference(x, L0_tok_W, L0_attn_W_qkv, L0_attn_b_qkv, L0_attn_W_out, L0_attn_b_out, L0_ffn_ln1_g, L0_ffn_ln1_b, L0_ffn_qkv_w, L0_ffn_proj_w, L0_ffn_proj_b, L0_ffn_ln2_g, L0_ffn_ln2_b, L0_ffn_gate_w, L0_ffn_gate_b, L0_ffn_w1, L0_ffn_b1, L0_ffn_w2, L0_ffn_b2):
    import jax
    import jax.numpy as jnp

    def _L0_tok_ref(x, W):
        import jax, jax.numpy as jnp
        import numpy as np
        CHANNEL = 3
        PATCH = 16
        D_MODEL = 192
        B, C, H, Wd = x.shape
        p = PATCH
        nH, nW = (H // p, Wd // p)
        patches = x.reshape(B, C, nH, p, nW, p)
        patches = patches.transpose(0, 2, 4, 3, 5, 1)
        flat = patches.reshape(B, nH * nW, p * p * C)
        return jnp.einsum('bnk,dk->bnd', flat, W)

    def _L0_attn_ref(x, W_qkv, b_qkv, W_out, b_out):
        import jax, jax.numpy as jnp
        import numpy as np
        FEATS = 192
        HEAD = 12
        HD = FEATS // HEAD
        B, N = (128, 197)
        b, n, f = x.shape
        h, hd = (W_qkv.shape[0], W_qkv.shape[1])
        xh = x.reshape(b, n, h, hd)
        qkv = jnp.einsum('bnhd,hde->bnhe', xh, W_qkv) + b_qkv
        q, k, v = jnp.split(qkv, 3, axis=-1)
        scale = jnp.asarray(f, x.dtype) ** 0.5
        scores = jnp.einsum('bihd,bjhd->bhij', q, k) / scale
        p = jax.nn.softmax(scores, axis=-1)
        attn = jnp.einsum('bhij,bjhd->bihd', p, v)
        out = attn.reshape(b, n, f) @ W_out + b_out
        return out

    def _L0_ffn_ref(x, ln1_g, ln1_b, qkv_w, proj_w, proj_b, ln2_g, ln2_b, gate_w, gate_b, w1, b1, w2, b2):
        import jax, jax.numpy as jnp
        import numpy as np
        B, N, DIM, HEADS = (4, 256, 192, 12)
        HIDDEN, E, TOPK = (768, 8, 2)
        EPS = 1e-05

        def _layernorm(x, g, b):
            mu = jnp.mean(x, axis=-1, keepdims=True)
            var = jnp.var(x, axis=-1, keepdims=True)
            return (x - mu) * jax.lax.rsqrt(var + EPS) * g + b
        b, n, d = x.shape
        hd = d // HEADS
        scale = hd ** (-0.5)
        h = _layernorm(x, ln1_g, ln1_b)
        qkv = h @ qkv_w.T
        qkv = qkv.reshape(b, n, 3, HEADS, hd).transpose(2, 0, 3, 1, 4)
        q, k, v = (qkv[0], qkv[1], qkv[2])
        attn = jax.nn.softmax(jnp.einsum('bhnd,bhmd->bhnm', q, k) * scale, axis=-1)
        a = jnp.einsum('bhnm,bhmd->bhnd', attn, v)
        a = a.transpose(0, 2, 1, 3).reshape(b, n, d)
        a = a @ proj_w.T + proj_b
        x = x + a
        h2 = _layernorm(x, ln2_g, ln2_b)
        t = h2.reshape(-1, d)
        T = t.shape[0]
        logits = t @ gate_w.T + gate_b
        top_val, top_idx = jax.lax.top_k(logits, TOPK)
        score = jax.nn.softmax(top_val, axis=-1)
        cw = jnp.zeros((T, E), t.dtype).at[jnp.arange(T)[:, None], top_idx].add(score)
        out = jnp.zeros_like(t)
        for e in range(E):
            he = jax.nn.gelu(t @ w1[e].T + b1[e], approximate=False)
            ye = he @ w2[e].T + b2[e]
            out = out + cw[:, e:e + 1] * ye
        return x + out.reshape(b, n, d)
    h = _L0_tok_ref(x, L0_tok_W)
    h = _layernorm(h + _L0_attn_ref(h, L0_attn_W_qkv, L0_attn_b_qkv, L0_attn_W_out, L0_attn_b_out), axis=-1)
    h = _layernorm(h + _L0_ffn_ref(h, L0_ffn_ln1_g, L0_ffn_ln1_b, L0_ffn_qkv_w, L0_ffn_proj_w, L0_ffn_proj_b, L0_ffn_ln2_g, L0_ffn_ln2_b, L0_ffn_gate_w, L0_ffn_gate_b, L0_ffn_w1, L0_ffn_b1, L0_ffn_w2, L0_ffn_b2), axis=-1)
    return h

_drawn_inputs = setup_inputs


def setup_inputs(seed=0):
    import zlib

    import numpy as np

    out = dict(_drawn_inputs(seed))
    spreads = {'L0_attn_b_qkv': (0.0, 0.1),
     'L0_attn_b_out': (0.0, 0.1),
     'L0_ffn_ln1_g': (1.0, 0.6),
     'L0_ffn_ln1_b': (0.0, 0.8),
     'L0_ffn_proj_b': (0.0, 0.1),
     'L0_ffn_ln2_g': (1.0, 0.6),
     'L0_ffn_ln2_b': (0.0, 0.637),
     'L0_ffn_gate_b': (0.0, 0.1),
     'L0_ffn_b1': (0.0, 0.738),
     'L0_ffn_b2': (0.0, 0.307)}
    factors = {'L0_attn_W_qkv': 3.87, 'L0_ffn_qkv_w': 3.957, 'L0_ffn_proj_w': 4.044}
    for name, (base, spread) in spreads.items():
        noise = np.random.default_rng([zlib.crc32(name.encode()), seed]).standard_normal(out[name].shape)
        drawn = base * np.exp(spread * noise) if base else spread * noise
        out[name] = jnp.asarray(drawn.astype(out[name].dtype))
    for name, factor in factors.items():
        out[name] = (out[name] * factor).astype(out[name].dtype)
    return out
```

```python
from contextlib import ExitStack

import numpy as np
import concourse.bass as bass
from concourse import mybir

ALU = mybir.AluOpType
ACT = mybir.ActivationFunctionType
AX_X = mybir.AxisListType.X
F32 = mybir.dt.float32
BF16 = mybir.dt.bfloat16
I32 = mybir.dt.int32
U32 = mybir.dt.uint32

P = 128
D = 192
T = 1024
NT = T // P
TG = 4
G = NT // TG
H, HD, N_IMG = 12, 16, 16
FC, NC_ = 96, 2
HC = FC // HD
QT = 32
KC = 3
HK = 4
KIN = 768 // P
E, HID = 8, 768
MH = HID // P
CAP = T
BLOCKS = (2 * T + E * (P - 1)) // P
EPS = 1e-5
NEG = -1e30

C_ID, C_U, C_ONE, C_MQ, C_MK, C_HM, C_IO, C_END = np.cumsum([0, P, P, P, P, H * QT, HC, BLOCKS + 1]).tolist()


def constants():
    c = np.zeros((P, C_END), np.float32)
    tok = np.arange(P)
    c[:, C_ID:C_ID + P] = np.eye(P)
    c[:, C_U:C_U + P] = tok[:, None] < tok[None, :]
    c[:, C_ONE:C_ONE + P] = 1.0
    for g in range(2):
        c[g, C_MQ:C_MQ + P] = (tok // N_IMG) % 2 == g
        c[g, C_MK:C_MK + H * QT] = np.where((np.arange(H * QT) % QT) // N_IMG == g, 0.0, NEG)
    for h in range(HC):
        c[h * HD:(h + 1) * HD, C_HM + h] = 1.0
    c[:, C_IO:C_END] = np.arange(BLOCKS + 1)
    return c


class Steps:

    def __init__(self, eng, sem, base=0):
        self.eng, self.sem, self.base, self.n = eng, sem, base, 0

    def done(self, ins):
        ins.then_inc(self.sem, 1)
        self.n += 1
        return self.n

    def join(self, n=None):
        self.eng.wait_ge(self.sem, self.base + (self.n if n is None else n))


def vit_block(nc, consts, x, w_tok, w_qkv1, small, w_out1, b_out1, w_qkv2, w_proj, b_proj, gate, gate_b,
              w1, b1, w2, b2, out):
    with ExitStack() as ctx:
        def sb(name, shape, dt=F32):
            return ctx.enter_context(nc.sbuf_tensor("sb_" + name, shape, dt))

        def sem(name):
            return ctx.enter_context(nc.semaphore(name))

        ps = ctx.enter_context(nc.psum_tensor("ps", [P, 8, 512], F32))
        rows_in = nc.dram_tensor("rows_in", [E * CAP, D], F32).ap()
        rows_out = nc.dram_tensor("rows_out", [BLOCKS * P, D], F32).ap()

        cst = sb("cst", [P, C_END])
        ident = cst[:, C_ID:C_ID + P]
        hmask = cst[:, C_HM:C_HM + HC]
        upper = sb("upper", [P, P], BF16)
        ones = sb("ones", [P, P], BF16)
        mask_q = sb("mask_q", [FC, P], BF16)
        mask_k = sb("mask_k", [FC, H * QT], BF16)
        minus_half = sb("minus_half", [P, 1])
        wtok = sb("wtok", [P, KIN, D])
        wqkv1 = sb("wqkv1", [FC, NC_, 3, FC])
        wqkv2 = sb("wqkv2", [FC, NC_, 3 * D])
        wout = [sb(f"wout{a}", [FC + 1, NC_, D]) for a in range(2)]
        wgate = sb("wgate", [FC + 1, NC_, E])
        col = sb("col", [FC, 7, NC_])
        b2s = sb("b2s", [P, E, D])
        w1s = sb("w1s", [FC + 1, E, NC_, HID])
        w2s = sb("w2s", [P, E, MH, D])
        tick = sb("tick", [P, 1])
        zero = sb("zero", [P, D])

        xin = sb("xin", [P, TG, KIN, P])
        hs = sb("hs", [P, TG, D])
        lnT = sb("lnT", [FC + 1, NC_, TG, P])
        aT = sb("aT", [FC + 1, TG, NC_, P])
        qk = sb("qk", [P, 2 * NC_ * TG * P])
        qT, kT = (qk[0:FC, i * NC_ * TG * P:(i + 1) * NC_ * TG * P].rearrange("p (c n) -> p c n", c=NC_) for i in range(2))
        big = sb("big", [P, NC_ * HC * TG * P])
        big2 = sb("big2", [P, TG * 4 * KC * HK * HD])
        kbd = big[0:FC].rearrange("p (c h n) -> p c h n", c=NC_, h=HC)
        vbd = big2[:].rearrange("p (t q c n) -> p t q c n", t=TG, q=4, c=KC)
        sc = sb("sc", [P, TG, H, QT])
        pT = sb("pT", [P, TG, KC, P])
        mx = sb("mx", [P, TG, H])
        sm = sb("sm", [P, TG, H])
        ri = sb("ri", [P, TG, H])
        at = sb("at", [P, TG, D])
        rs = at
        xh = sb("xh", [P, TG, D])
        st = sb("st", [P, TG, 6])
        mv = sb("mv", [P, TG, 2])
        ve = sb("ve", [P, TG, 1])
        rstd = sb("rstd", [P, TG, 1])
        lg = sb("lg", [P, TG, E])
        top = sb("top", [P, TG, E])
        tix = sb("tix", [P, TG, E], U32)
        tixf = sb("tixf", [P, TG, 2])
        dif = sb("dif", [P, TG, 1])
        exd = sb("exd", [P, TG, 1])
        den = sb("den", [P, TG, 1])
        hot = sb("hot", [P, TG, 2, E])
        hotb = sb("hotb", [P, TG, E], BF16)
        run = sb("run", [P, TG, E], BF16)
        pos = sb("pos", [P, TG, E])
        base = sb("base", [P, E])
        pick = sb("pick", [P, TG, 2, E])
        slf = sb("slf", [P, TG, 2])
        slf_all = sb("slf_all", [P, NT, 2])
        hot_all = sb("hot_all", [P, NT, 2, E])
        shift = sb("shift", [P, E])
        moved = sb("moved", [P, NT * 2, E])
        slot = sb("slot", [P, NT, 2], I32)
        slot_v = sb("slot_v", [P, TG, 2], I32)
        slot_g = sb("slot_g", [P, TG, 2], I32)
        wgt = sb("wgt", [P, NT, 2])
        xr = sb("xr", [P, NT, D])
        moved_sum = sb("moved_sum", [P, NT * 2])
        cnt = sb("cnt", [P, E])
        cmpb = sb("cmpb", [P, E, E])
        nblk = sb("nblk", [P, E])
        lastb = sb("lastb", [P, E])
        cmp2 = sb("cmp2", [P, BLOCKS, E])
        eof = sb("eof", [P, BLOCKS])
        cmp3 = sb("cmp3", [P, BLOCKS, E])
        fst = sb("fst", [P, BLOCKS])
        rowf = sb("rowf", [P, BLOCKS])
        tab_e = sb("tab_e", [P, BLOCKS], I32)
        tab_row = sb("tab_row", [P, BLOCKS], I32)
        xg = qk[:, 0:2 * D].rearrange("p (b d) -> p b d", b=2)
        yb = qk[:, 2 * D:4 * D].rearrange("p (b d) -> p b d", b=2)
        xgT = qk[0:FC + 1, 4 * D:4 * D + 2 * NC_ * P].rearrange("p (b c q) -> p b c q", b=2, c=NC_)
        w1c = big[0:FC + 1, 0:2 * NC_ * HID].rearrange("p (b c n) -> p b c n", b=2, c=NC_)
        hid = big[:, 2 * NC_ * HID:3 * NC_ * HID].rearrange("p (b m q) -> p b m q", b=2, m=MH)
        yg = big2[:, 0:8 * D].rearrange("p (n k d) -> p n k d", n=4, k=2)
        fo = big2[:, 8 * D:16 * D].rearrange("p (n d) -> p n d", n=NT)
        fs = big[:, 3 * NC_ * HID:3 * NC_ * HID + NT * D].rearrange("p (n d) -> p n d", n=NT)
        fst6 = sb("fst6", [P, NT, 6])
        fmv = sb("fmv", [P, NT, 2])
        fve = sb("fve", [P, NT, 1])
        frs = sb("frs", [P, NT, 1])

        s_const, s_wtok, s_small, s_wq1, s_w2nd = (sem(n) for n in ("s_const", "s_wtok", "s_small", "s_wq1", "s_w2nd"))
        s_x = [sem(f"s_x{t}") for t in range(TG)]
        s_moew = sem("s_moew")
        s_zero_tile, s_zeroed, s_prep, s_bd_zero = (sem(n) for n in ("s_zero_tile", "s_zeroed", "s_prep", "s_bd_zero"))
        s_tok, s_h, s_hT, s_lnT0 = (sem(n) for n in ("s_tok", "s_h", "s_hT", "s_lnT0"))

        names = ("k_mm k_ev q_mm q_ev kbd v_mm v_act v_dve score scaled prob pt_mm pt_ev av at at_mm at_ev "
                 "proj res ln_mm ln_ev var rstd").split()
        A = [{n: sem(f"s_{n}{a}") for n in names} for a in range(2)]
        var1, rstd1, x1n = sem("s_var1n"), sem("s_rstd1n"), sem("s_x1n")
        s_gate, s_dif, s_exd, s_hot, s_rank, s_slot, s_scat = (
            sem(n) for n in ("s_gate", "s_dif", "s_exd", "s_hot", "s_rank", "s_slot", "s_scat"))
        s_dve, s_pool, s_dve0, s_dve2, s_dve3, s_pool3 = (
            sem(n) for n in ("s_dve", "s_pool", "s_dve0", "s_dve2", "s_dve3", "s_pool3"))
        s_left, s_slots = sem("s_left"), sem("s_slots")
        s_cnt, s_tab, s_xg, s_xgfree = sem("s_cnt"), sem("s_tab"), [sem("s_xg0"), sem("s_xg1")], sem("s_xgfree")
        s_xgT, s_w1c, s_up, s_hid, s_down, s_y, s_st = (
            sem(n) for n in ("s_xgT", "s_w1c", "s_up", "s_hid", "s_down", "s_y", "s_st"))
        s_yst = [sem("s_yst0"), sem("s_yst1")]
        s_yg = [sem(f"s_yg{i}") for i in range(4)]
        s_mix, s_fvar, s_frs, s_fin, s_out = (sem(n) for n in ("s_mix", "s_fvar", "s_frs", "s_fin", "s_out"))

        block = ctx.enter_context(nc.Block())

        def bank(t, second=False):
            return ps[:, TG * second + t, :]

        def v_part(q, h):
            v = ps[QT * q:QT * q + QT, TG:2 * TG, 0:D]
            return v.rearrange("p t (c n) -> p t c n", c=KC)[:, :, :, HD * h:HD * h + HD]

        def vbd_part(q, h):
            return vbd[QT * h:QT * h + QT, :, q, :, HD * h:HD * h + HD]

        @block.sync
        def _(sp):
            def load_x(t, n):
                sp.dma_start(xin[:, t], x[n]).then_inc(s_x[t], 16)

            sp.dma_start(wtok[:], w_tok).then_inc(s_wtok, 16)
            load_x(0, 0)
            sp.dma_start(cst[:], consts).then_inc(s_const, 16)
            for t in range(1, TG):
                load_x(t, t)
            sp.wait_ge(s_bd_zero, 1)
            for h in range(H):
                c, r = h // HC, h % HC * HD
                sp.dma_start(wqkv1[r:r + HD, c, :, r:r + HD],
                             w_qkv1[h].rearrange("d (k e) -> d k e", k=3)).then_inc(s_wq1, 16)
            sp.dma_start(col[:], small).then_inc(s_small, 16)
            for src, bias, dst in ((w_out1, b_out1, wout[0]), (w_proj, b_proj, wout[1]), (gate, gate_b, wgate)):
                sp.dma_start(dst[0:FC], src).then_inc(s_w2nd, 16)
                sp.dma_start(dst[FC:FC + 1, NC_ - 1, :], bias).then_inc(s_w2nd, 16)
            sp.dma_start(wqkv2[:], w_qkv2).then_inc(s_w2nd, 16)
            sp.wait_ge(s_zero_tile, 1)
            for e in range(E):
                sp.dma_start(rows_in[e * CAP:(e + 1) * CAP].rearrange("(p r) d -> p r d", p=P),
                             zero[:].unsqueeze(1).broadcast_to([P, CAP // P, D])
                             ).then_inc(s_zeroed, 16)
            with sp.Fori(1, G) as g:
                for t in range(TG):
                    sp.wait_ge(s_tok, (g - 1) * TG + (t + 1))
                    load_x(t, g * TG + t)
            sp.dma_start(b2s[:], b2.partition_broadcast(P)).then_inc(s_moew, 16)
            for e in range(E):
                sp.dma_start(w1s[0:FC, e], w1[:, e]).then_inc(s_moew, 16)
                sp.dma_start(w1s[FC:FC + 1, e, NC_ - 1, :], b1[e:e + 1]).then_inc(s_moew, 16)
                sp.dma_start(w2s[:, e], w2[:, e]).then_inc(s_moew, 16)

            sp.wait_ge(s_tab, 1)
            sp.wait_ge(s_scat, 32 * NT)

            def row(i):
                return sp.value_load(tab_row[0:1, bass.ds(i, 1)], min_val=0, max_val=E * CAP - P)

            def load_rows(i, b):
                sp.dma_start(xg[:, b], rows_in[bass.ds(row(i), P)]).then_inc(s_xg[b], 16)

            def store_rows(i, b):
                sp.wait_ge(s_y, i + 1)
                sp.dma_start(rows_out[bass.ds(i * P, P)], yb[:, b]).then_inc(s_yst[b], 16)

            for b in range(2):
                load_rows(b, b)
            with sp.Fori(0, (BLOCKS - 3) // 2) as j:
                for b in range(2):
                    sp.wait_ge(s_xgfree, 2 * j + (b + 1))
                    load_rows(2 * j + b + 2, b)
                    store_rows(2 * j + b, b)
            j = (BLOCKS - 3) // 2
            sp.wait_ge(s_xgfree, 2 * j + 1)
            load_rows(2 * j + 2, 0)
            for i in range(2 * j, BLOCKS):
                store_rows(i, i % 2)
            for n in range(NT):
                sp.wait_ge(s_fin, n + 1)
                sp.dma_start(out[n * P:(n + 1) * P], fo[:, n]).then_inc(s_out, 16)
            sp.wait_ge(s_out, 16 * NT)

        @block.gpsimd
        def _(pool):
            nc.gpsimd.memset(minus_half[:], -0.5).then_inc(s_pool3, 1)
            pool.wait_ge(s_pool3, 1)
            nc.gpsimd.tensor_tensor(tick[:], minus_half[:], minus_half[:], ALU.add).then_inc(s_left, 1)
            pool.wait_ge(s_left, 1)

            def power(var_sem, out_sem, g, t, v, r, k=TG):
                pool.wait_ge(var_sem, g * k + (t + 1))
                nc.gpsimd.tensor_tensor(r, v, minus_half[:], ALU.pow).then_inc(out_sem, 1)

            with pool.Fori(0, G) as g:
                for v, r in ((A[0]["var"], A[0]["rstd"]), (var1, rstd1), (A[1]["var"], A[1]["rstd"])):
                    for t in range(TG):
                        power(v, r, g, t, ve[:, t], rstd[:, t])
                steps = Steps(pool, s_pool)
                pool.wait_ge(s_zeroed, 16 * E)
                for t in range(TG):
                    pool.wait_ge(s_slot, g * TG + (t + 1))
                    steps.done(nc.gpsimd.tensor_tensor(slot_g[:, t], slot_v[:, t],
                                                       zero[:, 0:2].bitcast(I32), ALU.add))
                    steps.join()
                    for k in range(2):
                        nc.gpsimd.indirect_dma_start(
                            out=rows_in, out_offset=bass.IndirectOffsetOnAxis(ap=slot_g[:, t, k:k + 1], axis=0),
                            in_=xh[:, t], in_offset=None).then_inc(s_scat, 16)
                pool.sem_clear(s_pool)
                pool.wait_ge(s_scat, (g + 1) * 32 * TG)
                nc.gpsimd.tensor_tensor(tick[:], minus_half[:], minus_half[:], ALU.add).then_inc(s_left, 1)
            for b in range(2):
                pool.wait_ge(s_yst[b], 16 * ((BLOCKS + 1 - b) // 2))

            pool.wait_ge(s_slots, 1)

            def gather(n):
                if n >= 4:
                    pool.wait_ge(s_mix, n - 3)
                for k in range(2):
                    nc.gpsimd.indirect_dma_start(
                        out=yg[:, n % 4, k], out_offset=None, in_=rows_out,
                        in_offset=bass.IndirectOffsetOnAxis(ap=slot[:, n, k:k + 1], axis=0)).then_inc(s_yg[n % 4], 16)

            for n in range(4):
                gather(n)
            for n in range(NT):
                power(s_fvar, s_frs, 0, n, fve[:, n], frs[:, n])
                if n + 4 < NT:
                    gather(n + 4)

        @block.scalar
        def _(act):
            act.wait_ge(s_small, 16)
            act.wait_ge(s_prep, 1)

            def attention(a, g):
                S = A[a]
                for i, (mm, ev, dst, bi) in enumerate((("k_mm", "k_ev", kT, 1), ("q_mm", "q_ev", qT, 0))):
                    for c in range(NC_):
                        act.wait_ge(S[mm], g * NC_ + (c + 1))
                        src = bank(2 * i + c)[0:FC]
                        if a == 0:
                            nc.scalar.activation(dst[:, c], src, ACT.Identity, bias=col[:, bi, c:c + 1]).then_inc(S[ev], 1)
                        else:
                            nc.scalar.activation(dst[:, c], src, ACT.Copy).then_inc(S[ev], 1)
                act.wait_ge(S["v_mm"], (g + 1) * TG)
                for q in range(2):
                    for h in range(HK):
                        ins = nc.scalar.activation(vbd_part(q, h), v_part(q, h), ACT.Copy)
                ins.then_inc(S["v_act"], 1)
                for t in range(TG):
                    act.wait_ge(S["scaled"], g * TG + (t + 1))
                    nc.scalar.activation(sc[:, t], sc[:, t], ACT.Exp,
                                         scale=[D ** -0.5, HD ** -0.5][a]).then_inc(S["prob"], 1)
                for t in range(TG):
                    act.wait_ge(S["pt_mm"], g * TG + (t + 1))
                    nc.scalar.activation(pT[:, t].rearrange("p c q -> p (c q)"), bank(t, True)[:, 0:KC * P],
                                         ACT.Copy).then_inc(S["pt_ev"], 1)
                for t in range(TG):
                    act.wait_ge(S["at_mm"], g * TG + (t + 1))
                    if a == 0:
                        for c in range(NC_):
                            ins = nc.scalar.activation(aT[0:FC, t, c], bank(t, True)[0:FC, c * P:(c + 1) * P],
                                                       ACT.Identity, bias=col[:, 2, c:c + 1])
                    else:
                        ins = nc.scalar.activation(aT[0:FC, t].rearrange("p c q -> p (c q)"),
                                                   bank(t, True)[0:FC, 0:NC_ * P], ACT.Copy)
                    ins.then_inc(S["at_ev"], 1)
                for t in range(TG):
                    act.wait_ge(S["ln_mm"], g * TG + (t + 1))
                    for c in range(NC_):
                        ins = nc.scalar.activation(lnT[0:FC, c, t], bank(t, True)[0:FC, c * P:(c + 1) * P], ACT.Identity,
                                                   scale=col[:, 3 + 2 * a, c:c + 1], bias=col[:, 4 + 2 * a, c:c + 1])
                    ins.then_inc(S["ln_ev"], 1)

            with act.Fori(0, G) as g:
                for t in range(TG):
                    act.wait_ge(s_tok, g * TG + (t + 1))
                    nc.scalar.activation(hs[:, t], bank(t)[:, 0:D], ACT.Copy).then_inc(s_h, 1)
                for t in range(TG):
                    act.wait_ge(s_hT, g * TG + (t + 1))
                    nc.scalar.activation(lnT[0:FC, :, t], bank(t, True)[0:FC, 0:NC_ * P].rearrange("p (c q) -> p c q", c=NC_),
                                         ACT.Copy).then_inc(s_lnT0, 1)
                attention(0, g)
                attention(1, g)
                for t in range(TG):
                    act.wait_ge(s_dif, g * TG + (t + 1))
                    nc.scalar.activation(exd[:, t], dif[:, t], ACT.Exp).then_inc(s_exd, 1)

            def turn(i, b):
                act.wait_ge(s_xgfree, i + 1)
                for c in range(NC_):
                    ins = nc.scalar.activation(xgT[0:FC, b, c], ps[0:FC, b, c * P:(c + 1) * P], ACT.Identity,
                                               scale=col[:, 5, c:c + 1], bias=col[:, 6, c:c + 1])
                ins.then_inc(s_xgT, 1)

            def gelu(i, b):
                act.wait_ge(s_up, i + 1)
                for u in range(2):
                    ins = nc.scalar.activation(hid[:, b, u * 3:u * 3 + 3].rearrange("p m q -> p (m q)"),
                                               ps[:, 2 + 2 * b + u, 0:3 * P], ACT.Gelu)
                ins.then_inc(s_hid, 1)

            turn(0, 0)
            gelu(0, 0)
            with act.Fori(0, (BLOCKS - 1) // 2) as j:
                for k in range(2):
                    turn(2 * j + (k + 1), 1 - k)
                    gelu(2 * j + (k + 1), 1 - k)

        @block.vector
        def _(dve):
            s0 = Steps(dve, s_dve0)
            s0.done(nc.vector.memset(wqkv1[:], 0.0))
            s0.join()
            nc.vector.tensor_copy(wqkv1[0:1, 0, 0, 0:1], wqkv1[0:1, 0, 0, 0:1]).then_inc(s_bd_zero, 1)
            nc.vector.memset(zero[:], 0.0).then_inc(s_zero_tile, 1)
            s0.done(nc.vector.memset(big2[:], 0.0))
            s0.done(nc.vector.memset(run[:], 0.0))
            s0.done(nc.vector.memset(lnT[FC:FC + 1], 1.0))
            s0.done(nc.vector.memset(aT[FC:FC + 1], 1.0))
            dve.wait_ge(s_const, 16)
            s0.done(nc.vector.tensor_copy(upper[:], cst[:, C_U:C_U + P]))
            s0.done(nc.vector.tensor_copy(ones[:], cst[:, C_ONE:C_ONE + P]))
            s0.done(nc.vector.tensor_copy(mask_q[:], cst[0:FC, C_MQ:C_MQ + P]))
            s0.done(nc.vector.tensor_copy(mask_k[:], cst[0:FC, C_MK:C_MK + H * QT]))
            s0.done(nc.vector.tensor_scalar(base[:], cst[:, C_IO:C_IO + E], float(CAP), None, ALU.mult))
            s0.join()
            nc.vector.tensor_copy(pos[:, 0], base[:]).then_inc(s_prep, 1)

            def normed(s, src, dst, g, t, var, rst, stats, mean_var, v, r, k=TG):
                s.done(nc.vector.bn_stats(stats, src))
                s.join()
                s.done(nc.vector.bn_aggr(mean_var, stats))
                s.join()
                nc.vector.tensor_scalar(v, mean_var[:, 1:2], EPS, None, ALU.add).then_inc(var, 1)

            def scale(s, src, dst, g, t, rst, mean_var, r, k=TG):
                dve.wait_ge(rst, g * k + (t + 1))
                s.done(nc.vector.tensor_scalar(dst, src, mean_var[:, 0:1], r, ALU.subtract, ALU.mult))

            def attention(a, g, s):
                S = A[a]
                for c in range(NC_):
                    dve.wait_ge(S["k_ev"], g * NC_ + (c + 1))
                    for h in range(HC):
                        ins = nc.vector.tensor_scalar(kbd[:, c, h], kT[:, c], hmask[0:FC, h:h + 1], None, ALU.mult)
                    ins.then_inc(S["kbd"], 1)
                dve.wait_ge(S["v_mm"], (g + 1) * TG)
                for q in range(2, 4):
                    for h in range(HK):
                        ins = nc.vector.tensor_copy(vbd_part(q, h), v_part(q, h))
                ins.then_inc(S["v_dve"], 1)
                for t in range(TG):
                    score = bank(t)[:, 0:H * QT].rearrange("p (h k) -> p h k", h=H)
                    dve.wait_ge(S["score"], g * TG + (t + 1))
                    s.done(nc.vector.tensor_reduce(mx[:, t], score, AX_X, ALU.max))
                    s.join()
                    nc.vector.tensor_tensor(sc[:, t], score, mx[:, t].unsqueeze(2).broadcast_to([P, H, QT]),
                                            ALU.subtract).then_inc(S["scaled"], 1)
                for t in range(TG):
                    dve.wait_ge(S["prob"], g * TG + (t + 1))
                    s.done(nc.vector.tensor_reduce(sm[:, t], sc[:, t], AX_X, ALU.add))
                    s.join()
                    s.done(nc.vector.reciprocal(ri[:, t], sm[:, t]))
                s.join()
                for t in range(TG):
                    dve.wait_ge(S["av"], g * TG + (t + 1))
                    nc.vector.tensor_tensor(at[:, t].rearrange("p (h d) -> p h d", h=H),
                                            bank(t)[:, 0:D].rearrange("p (h d) -> p h d", h=H),
                                            ri[:, t].unsqueeze(2).broadcast_to([P, H, HD]), ALU.mult).then_inc(S["at"], 1)
                for t in range(TG):
                    dve.wait_ge(S["proj"], g * TG + (t + 1))
                    s.done(nc.vector.tensor_tensor(rs[:, t], bank(t)[:, 0:D], hs[:, t], ALU.add))
                    s.join()
                    normed(s, rs[:, t], None, g, t, S["var"], None, st[:, t], mv[:, t], ve[:, t], None)
                if a == 0:
                    for t in range(TG):
                        scale(s, rs[:, t], hs[:, t], g, t, S["rstd"], mv[:, t], rstd[:, t])
                        s.join()
                        normed(s, hs[:, t], None, g, t, var1, None, st[:, t], mv[:, t], ve[:, t], None)
                    for t in range(TG):
                        dve.wait_ge(rstd1, g * TG + (t + 1))
                        nc.vector.tensor_scalar(xh[:, t], hs[:, t], mv[:, t, 0:1], rstd[:, t], ALU.subtract,
                                                ALU.mult).then_inc(S["res"], 1)
                else:
                    for t in range(TG):
                        dve.wait_ge(S["rstd"], g * TG + (t + 1))
                        nc.vector.tensor_scalar(xh[:, t], rs[:, t], mv[:, t, 0:1], rstd[:, t], ALU.subtract,
                                                ALU.mult).then_inc(S["res"], 1)
                        s.done(nc.vector.tensor_tensor(xr[:, bass.ds(g * TG + t, 1)].rearrange("p o d -> p (o d)"),
                                                       rs[:, t], hs[:, t], ALU.add))

            def route(g, s):
                io = cst[:, C_IO:C_IO + E]
                for t in range(TG):
                    dve.wait_ge(s_gate, g * TG + (t + 1))
                    s.done(nc.vector.tensor_copy(lg[:, t], bank(t)[:, 0:E]))
                    s.join()
                    s.done(nc.vector.max(top[:, t], lg[:, t]))
                    s.join()
                    nc.vector.tensor_tensor(dif[:, t], top[:, t, 1:2], top[:, t, 0:1], ALU.subtract).then_inc(s_dif, 1)
                    s.done(nc.vector.max_index(tix[:, t], top[:, t], lg[:, t]))
                    s.join()
                    s.done(nc.vector.tensor_copy(tixf[:, t], tix[:, t, 0:2]))
                    s.join()
                    for k in range(2):
                        s.done(nc.vector.tensor_scalar(hot[:, t, k], io, tixf[:, t, k:k + 1], None, ALU.is_equal))
                    s.join()
                    s.done(nc.vector.tensor_tensor(hotb[:, t], hot[:, t, 0], hot[:, t, 1], ALU.add))
                    s.join()
                    if t == TG - 1:
                        dve.wait_ge(s_rank, g * TG + 1)
                    nc.vector.tensor_tensor(run[:, (t + 1) % TG], run[:, t], hotb[:, t], ALU.add).then_inc(s_hot, 1)
                    dve.wait_ge(s_hot, g * TG + (t + 1))
                for t in range(TG):
                    n = g * TG + t
                    dve.wait_ge(s_rank, n + 1)
                    s.done(nc.vector.tensor_tensor(pos[:, t], bank(t, True)[:, 0:E], base[:], ALU.add))
                    s.join()
                    s.done(nc.vector.tensor_tensor(pick[:, t], hot[:, t],
                                                   pos[:, t].unsqueeze(1).broadcast_to([P, 2, E]), ALU.mult))
                    s.join()
                    s.done(nc.vector.tensor_reduce(slf[:, t], pick[:, t], AX_X, ALU.add))
                    s.join()
                    s.done(nc.vector.tensor_copy(slot_v[:, t], slf[:, t]))
                    s.join()
                    s.done(nc.vector.tensor_copy(hot_all[:, bass.ds(n, 1)].rearrange("p o k e -> p (o k) e"), hot[:, t]))
                    nc.vector.tensor_copy(slf_all[:, bass.ds(n, 1)].rearrange("p o k -> p (o k)"), slf[:, t]
                                          ).then_inc(s_slot, 1)
                    dve.wait_ge(s_exd, n + 1)
                    s.done(nc.vector.tensor_scalar(den[:, t], exd[:, t], 1.0, None, ALU.add))
                    s.join()
                    w = wgt[:, bass.ds(n, 1)].rearrange("p o k -> p (o k)")
                    s.done(nc.vector.reciprocal(w[:, 0:1], den[:, t]))
                    s.join()
                    s.done(nc.vector.tensor_tensor(w[:, 1:2], w[:, 0:1], exd[:, t], ALU.mult))

            with dve.Fori(0, G) as g:
                s = Steps(dve, s_dve)
                dve.wait_ge(s_left, g + 1)
                attention(0, g, s)
                attention(1, g, s)
                route(g, s)
                s.join()
                dve.sem_clear(s_dve)

            s2 = Steps(dve, s_dve2)
            rowf16 = moved_sum[:]
            io = cst[:, C_IO:C_IO + E]
            iob = cst[:, C_IO:C_IO + BLOCKS]
            dve.wait_ge(s_cnt, 1)
            s2.done(nc.vector.tensor_copy(cnt[:], ps[:, 2, 0:E]))
            s2.done(nc.vector.tensor_scalar(nblk[:], io, float(P), None, ALU.mult))
            s2.join()
            s2.done(nc.vector.tensor_tensor(cmpb[:], cnt[:].unsqueeze(2).broadcast_to([P, E, E]),
                                            nblk[:].unsqueeze(1).broadcast_to([P, E, E]), ALU.is_gt))
            s2.join()
            s2.done(nc.vector.tensor_reduce(nblk[:], cmpb[:], AX_X, ALU.add))
            s2.join()
            s2.done(nc.vector.tensor_copy(lastb[:], nblk[:]))
            for e in range(1, E):
                s2.join()
                s2.done(nc.vector.tensor_tensor(lastb[:, e:e + 1], lastb[:, e - 1:e], lastb[:, e:e + 1], ALU.add))
            s2.join()
            iob_e = iob.unsqueeze(2).broadcast_to([P, BLOCKS, E])
            last_e = lastb[:].unsqueeze(1).broadcast_to([P, BLOCKS, E])
            s2.done(nc.vector.tensor_tensor(cmp2[:], last_e, iob_e, ALU.is_le))
            s2.join()
            s2.done(nc.vector.tensor_reduce(eof[:], cmp2[:], AX_X, ALU.add))
            s2.done(nc.vector.tensor_tensor(cmp3[:], cmp2[:], nblk[:].unsqueeze(1).broadcast_to([P, BLOCKS, E]), ALU.mult))
            s2.join()
            s2.done(nc.vector.tensor_scalar(eof[:], eof[:], float(E - 1), None, ALU.min))
            s2.done(nc.vector.tensor_reduce(fst[:], cmp3[:], AX_X, ALU.add))
            s2.join()
            s2.done(nc.vector.tensor_tensor(fst[:], iob, fst[:], ALU.subtract))
            s2.join()
            s2.done(nc.vector.tensor_scalar(fst[:], fst[:], float(P), float(CAP - P), ALU.mult, ALU.min))
            s2.join()
            s2.done(nc.vector.scalar_tensor_tensor(out=rowf[:], in0=eof[:], scalar=float(CAP), in1=fst[:],
                                                   op0=ALU.mult, op1=ALU.add))
            s2.done(nc.vector.tensor_copy(tab_e[:], eof[:]))
            s2.join()
            s2.done(nc.vector.memset(xgT[FC:FC + 1], 1.0))
            s2.join()
            nc.vector.tensor_copy(tab_row[:], rowf[:]).then_inc(s_tab, 1)
            s2.done(nc.vector.tensor_tensor(shift[:], lastb[:], nblk[:], ALU.subtract))
            s2.join()
            s2.done(nc.vector.scalar_tensor_tensor(out=shift[:], in0=shift[:], scalar=float(P), in1=base[:],
                                                   op0=ALU.mult, op1=ALU.subtract))
            s2.join()
            s2.done(nc.vector.tensor_tensor(moved[:], hot_all[:].rearrange("p n k e -> p (n k) e"),
                                            shift[:].unsqueeze(1).broadcast_to([P, NT * 2, E]), ALU.mult))
            s2.join()
            slots = slf_all[:].rearrange("p n k -> p (n k)")
            s2.done(nc.vector.tensor_reduce(rowf16, moved[:], AX_X, ALU.add))
            s2.join()
            nc.vector.tensor_tensor(slot[:].rearrange("p n k -> p (n k)"), rowf16, slots, ALU.add).then_inc(s_slots, 1)
            dve.wait_ge(s_tab, 1)
            dve.wait_ge(s_moew, 16 * (1 + 3 * E))

            def expert(i):
                return dve.value_load(tab_e[0:1, bass.ds(i, 1)], min_val=0, max_val=E - 1)

            def stage_w1(i, b):
                e = expert(i)
                nc.vector.tensor_copy(w1c[0:FC, b, 0], w1s[0:FC, bass.ds(e, 1), 0].rearrange("p o n -> p (o n)"))
                nc.vector.tensor_copy(w1c[:, b, 1], w1s[:, bass.ds(e, 1), 1].rearrange("p o n -> p (o n)")
                                      ).then_inc(s_w1c, 1)

            def take_y(i, b, j, first):
                e = expert(i)
                dve.wait_ge(s_down, i + 1)
                if not first:
                    dve.wait_ge(s_yst[b], 16 * j)
                nc.vector.tensor_tensor(yb[:, b], ps[:, 6 + b, 0:D], b2s[:, bass.ds(e, 1)].rearrange("p o n -> p (o n)"),
                                        ALU.add).then_inc(s_y, 1)

            stage_w1(0, 0)
            stage_w1(1, 1)
            dve.wait_ge(s_up, 1)
            stage_w1(2, 0)
            take_y(0, 0, 0, True)
            dve.wait_ge(s_up, 2)
            stage_w1(3, 1)
            take_y(1, 1, 0, True)
            with dve.Fori(1, (BLOCKS - 3) // 2) as j:
                for b in range(2):
                    dve.wait_ge(s_up, 2 * j + (b + 1))
                    stage_w1(2 * j + b + 2, b)
                    take_y(2 * j + b, b, j, False)
            for i in range(BLOCKS - 3, BLOCKS):
                if i + 2 < BLOCKS:
                    dve.wait_ge(s_up, i + 1)
                    stage_w1(i + 2, i % 2)
                take_y(i, i % 2, i // 2, False)

            s3 = Steps(dve, s_dve3)
            for n in range(NT + 1):
                if n < NT:
                    dve.wait_ge(s_yg[n % 4], 32 * (n // 4 + 1))
                    s3.done(nc.vector.scalar_tensor_tensor(out=fs[:, n], in0=yg[:, n % 4, 0], scalar=wgt[:, n, 0:1],
                                                           in1=xr[:, n], op0=ALU.mult, op1=ALU.add))
                    s3.join()
                    s3.done(nc.vector.scalar_tensor_tensor(out=fs[:, n], in0=yg[:, n % 4, 1], scalar=wgt[:, n, 1:2],
                                                           in1=fs[:, n], op0=ALU.mult, op1=ALU.add))
                    s3.join()
                    s3.done(nc.vector.bn_stats(fst6[:, n], fs[:, n]))
                    s3.join()
                    nc.vector.bn_aggr(fmv[:, n], fst6[:, n]).then_inc(s_mix, 1)
                    dve.wait_ge(s_mix, n + 1)
                    nc.vector.tensor_scalar(fve[:, n], fmv[:, n, 1:2], EPS, None, ALU.add).then_inc(s_fvar, 1)
                if n >= 1:
                    dve.wait_ge(s_frs, n)
                    nc.vector.tensor_scalar(fo[:, n - 1], fs[:, n - 1], fmv[:, n - 1, 0:1], frs[:, n - 1], ALU.subtract,
                                            ALU.mult).then_inc(s_fin, 1)

        @block.tensor
        def _(pe):
            mm = nc.tensor.matmul
            tr = nc.tensor.transpose
            pe.wait_ge(s_const, 16)
            pe.wait_ge(s_prep, 1)
            pe.wait_ge(s_wtok, 16)

            def attention(a, g):
                S = A[a]
                src_ready = s_lnT0 if a == 0 else A[0]["ln_ev"]
                pe.wait_ge(src_ready, (g + 1) * TG)
                if a == 0:
                    pe.wait_ge(s_wq1, 16 * H)
                for i, (kind, name) in enumerate(((1, "k_mm"), (0, "q_mm"))):
                    for c in range(NC_):
                        dst = bank(2 * i + c)[0:FC]
                        if a == 0:
                            ins = mm(dst, wqkv1[:, c, kind], lnT[0:FC, c].rearrange("p t q -> p (t q)"), start=True, stop=True)
                        else:
                            for k in range(NC_):
                                ins = mm(dst, wqkv2[:, k, kind * D + c * FC:kind * D + (c + 1) * FC],
                                         lnT[0:FC, k].rearrange("p t q -> p (t q)"), start=(k == 0), stop=(k == NC_ - 1))
                        ins.then_inc(S[name], 1)
                for t in range(TG):
                    for c in range(NC_):
                        if a == 0:
                            ins = mm(bank(t, True)[:, c * FC:(c + 1) * FC], lnT[0:FC, c, t], wqkv1[:, c, 2], start=True, stop=True)
                        else:
                            ins = mm(bank(t, True)[:, 0:D], lnT[0:FC, c, t], wqkv2[:, c, 2 * D:3 * D],
                                     start=(c == 0), stop=(c == NC_ - 1))
                    ins.then_inc(S["v_mm"], 1)
                pe.wait_ge(S["q_ev"], (g + 1) * NC_)
                pe.wait_ge(S["kbd"], (g + 1) * NC_)
                for t in range(TG):
                    mm(bank(t)[:, 0:H * QT], mask_q[:], mask_k[:], start=True, stop=False, skip_group_check=True)
                    for c in range(NC_):
                        for q in range(4):
                            tok = slice(t * P + q * QT, t * P + (q + 1) * QT)
                            ins = mm(bank(t)[q * QT:(q + 1) * QT, c * HC * QT:(c + 1) * HC * QT], qT[:, c, tok],
                                     kbd[:, c, :, tok], start=False, stop=(c == NC_ - 1), skip_group_check=True)
                    ins.then_inc(S["score"], 1)
                pe.wait_ge(S["v_act"], g + 1)
                pe.wait_ge(S["v_dve"], g + 1)
                for t in range(TG):
                    pe.wait_ge(S["prob"], g * TG + (t + 1))
                    for c in range(KC):
                        ins = tr(bank(t, True)[:, c * P:(c + 1) * P], sc[:, t].rearrange("p h k -> p (h k)")[:, c * P:(c + 1) * P], ident)
                    ins.then_inc(S["pt_mm"], 1)
                for t in range(TG):
                    pe.wait_ge(S["pt_ev"], g * TG + (t + 1))
                    for c in range(KC):
                        for q in range(4):
                            ins = mm(bank(t)[q * QT:(q + 1) * QT, c * HK * HD:(c + 1) * HK * HD],
                                     pT[:, t, c, q * QT:(q + 1) * QT], vbd[:, t, q, c], start=True, stop=True)
                    ins.then_inc(S["av"], 1)
                for t in range(TG):
                    pe.wait_ge(S["at"], g * TG + (t + 1))
                    for c in range(NC_):
                        ins = tr(bank(t, True)[0:FC, c * P:(c + 1) * P], at[:, t, c * FC:(c + 1) * FC], ident)
                    ins.then_inc(S["at_mm"], 1)
                for t in range(TG):
                    pe.wait_ge(S["at_ev"], g * TG + (t + 1))
                    for c in range(NC_):
                        K = FC + (c == NC_ - 1)
                        ins = mm(bank(t)[:, 0:D], aT[0:K, t, c], wout[a][0:K, c], start=(c == 0), stop=(c == NC_ - 1))
                    ins.then_inc(S["proj"], 1)
                for t in range(TG):
                    pe.wait_ge(S["res"], g * TG + (t + 1))
                    for c in range(NC_):
                        ins = tr(bank(t, True)[0:FC, c * P:(c + 1) * P], xh[:, t, c * FC:(c + 1) * FC], ident)
                    ins.then_inc(S["ln_mm"], 1)

            with pe.Fori(0, G) as g:
                for t in range(TG):
                    pe.wait_ge(s_x[t], (g + 1) * 16)
                    for k in range(KIN):
                        ins = mm(bank(t)[:, 0:D], xin[:, t, k], wtok[:, k], start=(k == 0), stop=(k == KIN - 1))
                    ins.then_inc(s_tok, 1)
                for t in range(TG):
                    pe.wait_ge(s_h, g * TG + (t + 1))
                    for c in range(NC_):
                        ins = tr(bank(t, True)[0:FC, c * P:(c + 1) * P], hs[:, t, c * FC:(c + 1) * FC], ident)
                    ins.then_inc(s_hT, 1)
                pe.wait_ge(s_w2nd, 16 * 7)
                attention(0, g)
                attention(1, g)
                for t in range(TG):
                    pe.wait_ge(A[1]["ln_ev"], g * TG + (t + 1))
                    for c in range(NC_):
                        K = FC + (c == NC_ - 1)
                        ins = mm(bank(t)[:, 0:E], lnT[0:K, c, t], wgate[0:K, c], start=(c == 0), stop=(c == NC_ - 1))
                    ins.then_inc(s_gate, 1)
                for t in range(TG):
                    pe.wait_ge(s_hot, g * TG + (t + 1))
                    mm(bank(t, True)[:, 0:E], upper[:], hotb[:, t], start=True, stop=False)
                    mm(bank(t, True)[:, 0:E], ones[:], run[:, t], start=False, stop=True).then_inc(s_rank, 1)
                pe.wait_ge(s_slot, (g + 1) * TG)
            mm(ps[:, 2, 0:E], ones[:], run[:, 0], start=True, stop=True).then_inc(s_cnt, 1)

            pe.wait_ge(s_tab, 1)
            pe.wait_ge(s_moew, 16 * (1 + 3 * E))

            def up(i, b, j):
                pe.wait_ge(s_xg[b], 16 * (j + 1))
                for c in range(NC_):
                    ins = tr(ps[0:FC, b, c * P:(c + 1) * P], xg[:, b, c * FC:(c + 1) * FC], ident)
                ins.then_inc(s_xgfree, 1)
                pe.wait_ge(s_w1c, i + 1)
                pe.wait_ge(s_xgT, i + 1)
                for m in range(MH):
                    for c in range(NC_):
                        K = FC + (c == NC_ - 1)
                        ins = mm(ps[:, 2 + 2 * b + m // 3, m % 3 * P:(m % 3 + 1) * P], w1c[0:K, b, c, m * P:(m + 1) * P],
                                 xgT[0:K, b, c], start=(c == 0), stop=(c == NC_ - 1))
                ins.then_inc(s_up, 1)

            def down(i, b):
                e = pe.value_load(tab_e[0:1, bass.ds(i, 1)], min_val=0, max_val=E - 1)
                pe.wait_ge(s_hid, i + 1)
                for m in range(MH):
                    ins = mm(ps[:, 6 + b, 0:D], hid[:, b, m], w2s[:, bass.ds(e, 1), m].rearrange("p o n -> p (o n)"),
                             start=(m == 0), stop=(m == MH - 1))
                ins.then_inc(s_down, 1)

            up(0, 0, 0)
            with pe.Fori(0, (BLOCKS - 1) // 2) as j:
                up(2 * j + 1, 1, j)
                down(2 * j, 0)
                up(2 * j + 2, 0, j + 1)
                down(2 * j + 1, 1)
            pe.wait_ge(s_y, BLOCKS - 2)
            down(BLOCKS - 1, 0)


def kernel(x, L0_tok_W, L0_attn_W_qkv, L0_attn_b_qkv, L0_attn_W_out, L0_attn_b_out, L0_ffn_ln1_g, L0_ffn_ln1_b,
           L0_ffn_qkv_w, L0_ffn_proj_w, L0_ffn_proj_b, L0_ffn_ln2_g, L0_ffn_ln2_b, L0_ffn_gate_w, L0_ffn_gate_b,
           L0_ffn_w1, L0_ffn_b1, L0_ffn_w2, L0_ffn_b2):
    import concourse.bacc as bacc
    from concourse.bass_utils import run_bass_kernel_spmd

    def laid(a):
        return np.ascontiguousarray(a)

    def chunks(w):
        return laid(np.asarray(w).reshape(NC_, FC, -1).transpose(1, 0, 2))

    n_img, side, p = x.shape[0], x.shape[2] // 16, 16
    patches = np.asarray(x).reshape(n_img, 3, side, p, side, p).transpose(0, 2, 4, 3, 5, 1)
    patches = patches.reshape(NT, P, KIN, P).transpose(0, 3, 2, 1)
    b_qkv = np.asarray(L0_attn_b_qkv).reshape(H, 3, HD).transpose(1, 0, 2).reshape(3, NC_, FC)
    lns = [np.asarray(v).reshape(1, NC_, FC) for v in (L0_ffn_ln1_g, L0_ffn_ln1_b, L0_ffn_ln2_g, L0_ffn_ln2_b)]
    arrays = {
        "consts": constants(),
        "patches": laid(patches),
        "w_tok": laid(np.asarray(L0_tok_W).T.reshape(KIN, P, D).transpose(1, 0, 2)),
        "w_qkv1": laid(L0_attn_W_qkv),
        "small": laid(np.concatenate([b_qkv, *lns]).transpose(2, 0, 1)),
        "w_out1": chunks(L0_attn_W_out),
        "b_out1": laid(np.asarray(L0_attn_b_out).reshape(1, D)),
        "w_qkv2": chunks(np.asarray(L0_ffn_qkv_w).T),
        "w_proj": chunks(np.asarray(L0_ffn_proj_w).T),
        "b_proj": laid(np.asarray(L0_ffn_proj_b).reshape(1, D)),
        "gate": chunks(np.asarray(L0_ffn_gate_w).T),
        "gate_b": laid(np.asarray(L0_ffn_gate_b).reshape(1, E)),
        "w1": laid(np.asarray(L0_ffn_w1).transpose(2, 0, 1).reshape(NC_, FC, E, HID).transpose(1, 2, 0, 3)),
        "b1": laid(L0_ffn_b1),
        "w2": laid(np.asarray(L0_ffn_w2).transpose(2, 0, 1).reshape(MH, P, E, D).transpose(1, 2, 0, 3)),
        "b2": laid(L0_ffn_b2),
    }
    nc = bacc.Bacc("TRN2", target_bir_lowering=False, num_devices=1)
    args = [nc.dram_tensor(k, a.shape, mybir.dt.from_np(a.dtype), kind="ExternalInput").ap() for k, a in arrays.items()]
    out = nc.dram_tensor("out", (T, D), F32, kind="ExternalOutput").ap()
    vit_block(nc, *args, out)
    got = run_bass_kernel_spmd(nc, [arrays], core_ids=[0]).results[0]["out"]
    return got.reshape(n_img, side * side, D)
```

```python
from contextlib import ExitStack

import numpy as np
import concourse.bass as bass
from concourse import mybir

ALU = mybir.AluOpType
ACT = mybir.ActivationFunctionType
AX_X = mybir.AxisListType.X
F32 = mybir.dt.float32
BF16 = mybir.dt.bfloat16
I32 = mybir.dt.int32
U32 = mybir.dt.uint32

P = 128
D = 192
T = 1024
NT = T // P
TG = 4
G = NT // TG
PAIRS, TP = 2, 2
H, HD, N_IMG = 12, 16, 16
FC, NC_ = 96, 2
HC = FC // HD
ACT_HEADS = 2
QT = 32
KC = 3
HK = 4
KIN = 768 // P
E, HID = 8, 768
MH = HID // P
CAP = T
RW = D + E + 1
XB = 4
BLOCKS = (2 * T + E * (P - 1)) // P
LQ = 4
HN = NT // LQ
EPS = 1e-5
NEG = -1e30

ORDER = [(stage[:-1], "AB".index(stage[-1])) for stage in (
    "tokA tokB turnA turnB qk0A qk0B v0A score0A v0B pt0A score0B av0A at0A pt0B proj0A av0B norm0A at0B ln0A proj0B qk1A norm0B "
    "v1A ln0B score1A qk1B pt1A v1B score1B av1A pt1B at1A av1B proj1A norm1A at1B proj1B ln1A norm1B gateA ln1B rankA gateB rankB").split()]

C_ID, C_U, C_MQ, C_MK, C_HM, C_IO, C_TOK, C_END = np.cumsum(
    [0, P, P, P, H * QT, HC, BLOCKS + 1, TG + 1]).tolist()


def constants():
    c = np.zeros((P, C_END), np.float32)
    tok = np.arange(P)
    c[:, C_ID:C_ID + P] = np.eye(P)
    c[:, C_U:C_U + P] = tok[:, None] < tok[None, :]
    for g in range(2):
        c[g, C_MQ:C_MQ + P] = (tok // N_IMG) % 2 == g
        c[g, C_MK:C_MK + H * QT] = np.where((np.arange(H * QT) % QT) // N_IMG == g, 0.0, NEG)
    for h in range(HC):
        c[h * HD:(h + 1) * HD, C_HM + h] = 1.0
    c[:, C_IO:C_TOK] = np.arange(BLOCKS + 1)
    c[:, C_TOK:C_TOK + TG] = tok[:, None] + P * np.arange(TG)
    c[:, C_TOK + TG] = T + tok
    return c


class Steps:

    def __init__(self, eng, sem, base=0):
        self.eng, self.sem, self.base, self.n = eng, sem, base, 0

    def done(self, ins):
        ins.then_inc(self.sem, 1)
        self.n += 1
        return self.n

    def join(self, n=None):
        self.eng.wait_ge(self.sem, self.base + (self.n if n is None else n))


def vit_block(nc, consts, x, w_tok, w_qkv1, b_qkv1, ln_gb, w_out1, b_out1, w_qkv2, w_proj, b_proj, gate, gate_b,
              w1, b1, w2, b2, out):
    with ExitStack() as ctx:
        def sb(name, shape, dt=F32):
            return ctx.enter_context(nc.sbuf_tensor("sb_" + name, shape, dt))

        def sem(name):
            return ctx.enter_context(nc.semaphore(name))

        ps = ctx.enter_context(nc.psum_tensor("ps", [P, 8, 512], F32))
        rows_in = nc.dram_tensor("rows_in", [E * CAP + P, RW], F32).ap()
        acc = nc.dram_tensor("acc", [T + P, D], F32).ap()

        cst = sb("cst", [P, C_END])
        ident = cst[:, C_ID:C_ID + P]
        hmask = cst[:, C_HM:C_HM + HC]
        upper = sb("upper", [P, P], BF16)
        ones = sb("ones", [P, P], BF16)
        mask_q = sb("mask_q", [FC, P], BF16)
        mask_k = sb("mask_k", [FC, H * QT], BF16)
        minus_half = sb("minus_half", [P, 2 * TP])
        wtok = sb("wtok", [P, KIN, D])
        wqkv1 = sb("wqkv1", [FC + 1, NC_, 3, FC])
        wqkv2 = sb("wqkv2", [FC, NC_, 3 * D])
        wout = [sb(f"wout{a}", [FC + 1, NC_, D]) for a in range(2)]
        wgate = sb("wgate", [FC + 1, NC_, E])
        col = sb("col", [FC, 4, NC_])
        b2s = sb("b2s", [P, E, D])
        w1s = sb("w1s", [FC + 1, E, NC_, HID])
        w2s = sb("w2s", [P, E, MH, D])
        tick = sb("tick", [P, 1])
        warm_act = sb("warm_act", [P, 1])
        empty = sb("empty", [P, RW])

        xin = sb("xin", [P, TG, KIN, P])
        hs = sb("hs", [P, TG, D])
        lnT = sb("lnT", [FC + 1, NC_, TG, P])
        aT = sb("aT", [FC + 1, TG, NC_, P])
        qk = sb("qk", [P, 2 * NC_ * TG * P])
        qT, kT = (qk[0:FC, i * NC_ * TG * P:(i + 1) * NC_ * TG * P].rearrange("p (c n) -> p c n", c=NC_) for i in range(2))
        big = sb("big", [P, NC_ * HC * TG * P])
        big2 = sb("big2", [P, TG * 4 * KC * HK * HD])
        kbd = big[0:FC].rearrange("p (c h n) -> p c h n", c=NC_, h=HC)
        vbd = big2[:].rearrange("p (t q c n) -> p t q c n", t=TG, q=4, c=KC)
        sc = sb("sc", [P, TG, H, QT])
        xh = sc[:].rearrange("p t h k -> p t (h k)")[:, :, 0:D]
        pT = sb("pT", [P, TG, KC, P])
        mx = sb("mx", [P, TG, H])
        sm = sb("sm", [P, TG, H])
        ri = sb("ri", [P, TG, H])
        at = sb("at", [P, TG, D])
        rs = at
        xd = sb("xd", [P, TG, RW])
        st = sb("st", [P, TG, 6])
        mv = sb("mv", [P, TG, 2])
        ve = sb("ve", [P, PAIRS, 2, TP])
        rstd = sb("rstd", [P, PAIRS, 2, TP])
        both = sb("both", [P, PAIRS, TP])
        lg = sb("lg", [P, TG, E])
        top = sb("top", [P, TG, E])
        tix = sb("tix", [P, TG, E], U32)
        tixf = sb("tixf", [P, TG, 2])
        dif = sb("dif", [P, TG, 1])
        exd = sb("exd", [P, TG, 1])
        den = sb("den", [P, TG, 1])
        hot = sb("hot", [P, TG, 2, E])
        hotb = sb("hotb", [P, TG, E], BF16)
        run = sb("run", [P, E], BF16)
        pos = sb("pos", [P, TG, E])
        base = sb("base", [P, E])
        pick = sb("pick", [P, TG, 2, E])
        slf = sb("slf", [P, TG, 2])
        slot_v = sb("slot_v", [P, TG, 2], I32)
        slot_g = sb("slot_g", [P, TG, 2], I32)
        w01 = sb("w01", [P, TG, 2])
        hw = sb("hw", [P, TG, 2, E])
        toks = sb("toks", [P, TG])
        xr = sb("xr", [P, NT, D])
        cnt = sb("cnt", [P, E])
        cmpb = sb("cmpb", [P, E, E])
        nblk = sb("nblk", [P, E])
        lastb = sb("lastb", [P, E])
        cmp2 = sb("cmp2", [P, BLOCKS, E])
        eof = sb("eof", [P, BLOCKS])
        cmp3 = sb("cmp3", [P, BLOCKS, E])
        fst = sb("fst", [P, BLOCKS])
        rowf = sb("rowf", [P, BLOCKS])
        tab_e = sb("tab_e", [P, BLOCKS], I32)
        tab_row = sb("tab_row", [P, BLOCKS], I32)
        xg = qk[:, 0:XB * RW].rearrange("p (b d) -> p b d", b=XB)
        o = XB * RW
        yb = qk[:, o:o + 2 * D].rearrange("p (b d) -> p b d", b=2)
        o += 2 * D
        xgT = qk[0:FC + 1, o:o + 2 * NC_ * P].rearrange("p (b c q) -> p b c q", b=2, c=NC_)
        tok_g = sb("tok_g", [P, 2, 1], I32)
        w1c = big[0:FC + 1, 0:2 * NC_ * HID].rearrange("p (b c n) -> p b c n", b=2, c=NC_)
        hid = big[:, 2 * NC_ * HID:3 * NC_ * HID].rearrange("p (b m q) -> p b m q", b=2, m=MH)
        fo = big2[:, 0:NT * D].rearrange("p (n d) -> p n d", n=NT)
        fs = big[:, 3 * NC_ * HID:3 * NC_ * HID + NT * D].rearrange("p (n d) -> p n d", n=NT)
        fst6 = sb("fst6", [P, NT, 6])
        fmv = sb("fmv", [P, NT, 2])
        fve = sb("fve", [P, NT])
        frs = sb("frs", [P, NT])
        off = sb("off", [P, NT])

        s_const, s_wtok, s_small, s_wq1, s_w2nd = (sem(n) for n in ("s_const", "s_wtok", "s_small", "s_wq1", "s_w2nd"))
        s_x = [sem(f"s_x{t}") for t in range(TG)]
        s_moew = sem("s_moew")
        s_ones, s_zero_tile, s_zeroed, s_prep, s_bd_zero = (sem(n) for n in ("s_ones", "s_zero_tile", "s_zeroed", "s_prep", "s_bd_zero"))

        def per_pair(*names):
            return [{n: sem(f"s_{n}_{'ab'[p]}") for n in names} for p in range(PAIRS)]

        TOK = per_pair(*"tok h hT lnT gate dif exd hot rank slot".split())
        names = ("k_mm k_ev q_mm q_ev kbd v_mm v_act v_dve score scaled prob pt_mm pt_ev av at at_mm at_ev "
                 "proj res ln_mm ln_ev var rstd").split()
        ATT = per_pair(*names)
        s_counted, s_scat, s_run = sem("s_counted"), sem("s_scat"), sem("s_run")
        s_dve, s_pool, s_dve0, s_dve2, s_dve3, s_pool3 = (
            sem(n) for n in ("s_dve", "s_pool", "s_dve0", "s_dve2", "s_dve3", "s_pool3"))
        s_left, s_xr, s_acc = sem("s_left"), sem("s_xr"), sem("s_acc")
        s_cnt, s_tab, s_xg, s_xgfree = sem("s_cnt"), sem("s_tab"), [sem(f"s_xg{b}") for b in range(XB)], sem("s_xgfree")
        s_xgT, s_w1c, s_up, s_hid, s_down, s_y, s_tok_g, s_add, s_dve4 = (
            sem(n) for n in ("s_xgT", "s_w1c", "s_up", "s_hid", "s_down", "s_y", "s_tok_g", "s_add", "s_dve4"))
        s_fs = [sem(f"s_fs{u}") for u in range(LQ)]
        s_fvar, s_frs, s_off, s_fin, s_fin_a, s_out = (sem(n) for n in ("s_fvar", "s_frs", "s_off", "s_fin", "s_fin_a", "s_out"))

        block = ctx.enter_context(nc.Block())

        def bank(t, second=False):
            return ps[:, TG * second + t, :]

        def banks(p, second=False):
            return ps[:, TG * second + TP * p:TG * second + TP * p + TP, :]

        def v_part(p, q, h):
            v = ps[QT * q:QT * q + QT, TG + TP * p:TG + TP * p + TP, 0:D]
            return v.rearrange("p t (c n) -> p t c n", c=KC)[:, :, :, HD * h:HD * h + HD]

        def vbd_part(p, q, h):
            return vbd[QT * h:QT * h + QT, TP * p:TP * p + TP, q, :, HD * h:HD * h + HD]

        def tiles(p):
            return slice(TP * p, TP * p + TP)

        def tokens(p):
            return slice(TP * p * P, (TP * p + TP) * P)

        def part(tile, u):
            return tile[:, u * HN:(u + 1) * HN]

        def part_rows(rows, u):
            return rows[u * HN * P:(u + 1) * HN * P].rearrange("(n p) d -> p n d", p=P)

        @block.sync
        def _(sp):
            def load_x(t, n):
                sp.dma_start(xin[:, t], x[n]).then_inc(s_x[t], 16)

            for k in range(0, KIN, KIN // 2):
                half = slice(k, k + KIN // 2)
                sp.dma_start(wtok[:, half], w_tok[:, half]).then_inc(s_wtok, 16)
                sp.dma_start(xin[:, 0, half], x[0, :, half]).then_inc(s_x[0], 16)
            sp.dma_start(cst[:], consts).then_inc(s_const, 16)
            for t in range(1, TG):
                load_x(t, t)
            sp.wait_ge(s_bd_zero, 1)
            for h in range(H):
                c, r = h // HC, h % HC * HD
                sp.dma_start(wqkv1[r:r + HD, c, :, r:r + HD],
                             w_qkv1[h].rearrange("d (k e) -> d k e", k=3)).then_inc(s_wq1, 16)
            sp.dma_start(wqkv1[FC:FC + 1], b_qkv1).then_inc(s_wq1, 16)
            sp.dma_start(col[:], ln_gb).then_inc(s_small, 16)
            for src, bias, dst in ((w_out1, b_out1, wout[0]), (w_proj, b_proj, wout[1]), (gate, gate_b, wgate)):
                sp.dma_start(dst[0:FC], src).then_inc(s_w2nd, 16)
                sp.dma_start(dst[FC:FC + 1, NC_ - 1, :], bias).then_inc(s_w2nd, 16)
            sp.dma_start(wqkv2[:], w_qkv2).then_inc(s_w2nd, 16)
            sp.wait_ge(s_zero_tile, 1)
            for e in range(E + 1):
                last = min((e + 1) * CAP, E * CAP + P)
                sp.dma_start(rows_in[e * CAP:last].rearrange("(r p) d -> p r d", p=P),
                             empty[:].unsqueeze(1).broadcast_to([P, (last - e * CAP) // P, RW])
                             ).then_inc(s_zeroed, 16)
            sp.dma_start(acc[T:T + P], empty[:, 0:D]).then_inc(s_acc, 16)
            with sp.Fori(1, G) as g:
                for t in range(TG):
                    sp.wait_ge(TOK[t // TP]["tok"], (g - 1) * TP + (t % TP + 1))
                    load_x(t, g * TG + t)
            sp.dma_start(b2s[:], b2.partition_broadcast(P)).then_inc(s_moew, 16)
            for e in range(E):
                sp.dma_start(w1s[0:FC, e], w1[:, e]).then_inc(s_moew, 16)
                sp.dma_start(w1s[FC:FC + 1, e, NC_ - 1, :], b1[e:e + 1]).then_inc(s_moew, 16)
                sp.dma_start(w2s[:, e], w2[:, e]).then_inc(s_moew, 16)

            sp.wait_ge(s_xr, G * PAIRS)
            sp.dma_start(acc[0:T].rearrange("(n p) d -> p n d", p=P), xr[:]).then_inc(s_acc, 16)

            sp.wait_ge(s_tab, 1)
            sp.wait_ge(s_scat, 32 * NT)

            def load_rows(i, b):
                first = sp.value_load(tab_row[0:1, bass.ds(i, 1)], min_val=0, max_val=E * CAP)
                sp.dma_start(xg[:, b], rows_in[bass.ds(first, P)]).then_inc(s_xg[b], 16)

            for b in range(XB):
                load_rows(b, b)
            with sp.Fori(1, BLOCKS // XB) as j:
                for b in range(XB):
                    sp.wait_ge(s_tok_g, XB * j + (b + 1 - XB))
                    load_rows(XB * j + b, b)
            for i in range(BLOCKS // XB * XB, BLOCKS):
                sp.wait_ge(s_tok_g, i + 1 - XB)
                load_rows(i, i % XB)

            sp.wait_ge(s_add, 16 * BLOCKS)
            for u in range(0, LQ, 2):
                sp.dma_start(part(fs, u), part_rows(acc, u)).then_inc(s_fs[u], 16)
            for u in range(LQ):
                sp.wait_ge(s_fin, u + 1)
                sp.wait_ge(s_fin_a, u + 1)
                sp.dma_start(part_rows(out, u), part(fo, u)).then_inc(s_out, 16)
            sp.wait_ge(s_out, 16 * LQ)

        @block.gpsimd
        def _(pool):
            nc.gpsimd.memset(minus_half[:], -0.5).then_inc(s_pool3, 1)
            pool.wait_ge(s_pool3, 1)
            nc.gpsimd.tensor_tensor(tick[:], minus_half[:, 0:1], minus_half[:, 0:1], ALU.add).then_inc(s_left, 1)
            pool.wait_ge(s_left, 1)

            def power(ready, count, done, v, r):
                pool.wait_ge(ready, count)
                nc.gpsimd.tensor_tensor(r, v, minus_half[:, 0:v.shape[1]], ALU.pow).then_inc(done, 1)

            def dispatch(p, g, steps):
                pool.wait_ge(s_zeroed, 16 * (E + 1))
                pool.wait_ge(TOK[p]["slot"], g + 1)
                steps.done(nc.gpsimd.tensor_tensor(slot_g[:, tiles(p)], slot_v[:, tiles(p)],
                                                   empty[:, 0:2 * TP].bitcast(I32).rearrange("p (t k) -> p t k", k=2), ALU.add))
                steps.join()
                for t in range(TP * p, TP * p + TP):
                    for k in range(2):
                        nc.gpsimd.indirect_dma_start(
                            out=rows_in, out_offset=bass.IndirectOffsetOnAxis(ap=slot_g[:, t, k:k + 1], axis=0),
                            in_=xd[:, t], in_offset=None).then_inc(s_scat, 16)

            with pool.Fori(0, G) as g:
                steps = Steps(pool, s_pool)
                for stage, p in ORDER:
                    if stage == "proj0":
                        power(ATT[p]["var"], g * 2 + 1, ATT[p]["rstd"], ve[:, p].rearrange("p l t -> p (l t)"),
                              rstd[:, p].rearrange("p l t -> p (l t)"))
                    if stage == "proj1":
                        power(ATT[p]["var"], g * 2 + 2, ATT[p]["rstd"], ve[:, p, 0], rstd[:, p, 0])
                    if stage == "rank":
                        dispatch(p, g, steps)
                pool.sem_clear(s_pool)
                pool.wait_ge(s_scat, (g + 1) * 32 * TG)
                nc.gpsimd.tensor_tensor(tick[:], minus_half[:, 0:1], minus_half[:, 0:1], ALU.add).then_inc(s_left, 1)

            def add_rows(i, b, xb, k, first=False):
                pool.wait_ge(s_y, i + 1)
                if not first:
                    pool.wait_ge(s_add, 16 * i)
                nc.gpsimd.tensor_tensor(tok_g[:, b], xg[:, xb, RW - 1:RW].bitcast(I32), empty[:, 0:1].bitcast(I32),
                                        ALU.add).then_inc(s_tok_g, 1)
                pool.wait_ge(s_tok_g, i + 1)
                nc.gpsimd.tensor_tensor(tick[:], minus_half[:, 0:1], minus_half[:, 0:1], ALU.add).then_inc(s_pool, 1)
                pool.wait_ge(s_pool, k)
                nc.gpsimd.indirect_dma_start(
                    out=acc, out_offset=bass.IndirectOffsetOnAxis(ap=tok_g[:, b], axis=0),
                    in_=yb[:, b], in_offset=None, compute_op=ALU.add).then_inc(s_add, 16)

            pool.wait_ge(s_acc, 16 * 2)
            add_rows(0, 0, 0, 1, first=True)
            for i in range(1, XB):
                add_rows(i, i % 2, i, i + 1)
            pool.sem_clear(s_pool)
            with pool.Fori(1, BLOCKS // XB) as j:
                for b in range(XB):
                    add_rows(XB * j + b, b % 2, b, b + 1)
                pool.sem_clear(s_pool)
            for i in range(BLOCKS // XB * XB, BLOCKS):
                add_rows(i, i % 2, i % XB, i % XB + 1)
            for u in range(LQ):
                power(s_fvar, u + 1, s_frs, part(fve, u), part(frs, u))

        @block.scalar
        def _(act):
            act.wait_ge(s_small, 16)
            act.wait_ge(s_prep, 1)

            def take_h(p, g):
                act.wait_ge(TOK[p]["tok"], (g + 1) * TP)
                nc.scalar.activation(hs[:, tiles(p)], banks(p)[:, :, 0:D], ACT.Copy).then_inc(TOK[p]["h"], 1)

            def take_turned(p, g):
                act.wait_ge(TOK[p]["hT"], g + 1)
                nc.scalar.activation(lnT[0:FC, :, tiles(p)].rearrange("p c t q -> p t c q"),
                                     banks(p, True)[0:FC, :, 0:NC_ * P].rearrange("p t (c q) -> p t c q", c=NC_),
                                     ACT.Copy).then_inc(TOK[p]["lnT"], 1)

            def take_qk(a, p, r):
                S = ATT[p]
                for mm, ev, dst, b in (("k_mm", "k_ev", kT, 0), ("q_mm", "q_ev", qT, 1)):
                    act.wait_ge(S[mm], r + 1)
                    src = bank(TP * p + b)[0:FC].rearrange("p (c n) -> p c n", c=NC_)
                    nc.scalar.activation(dst[:, :, tokens(p)], src, ACT.Copy).then_inc(S[ev], 1)
                    if b == 0:
                        for h in range(HC - ACT_HEADS, HC):
                            nc.scalar.activation(kbd[:, :, h, tokens(p)], src, ACT.Copy, scale=hmask[0:FC, h:h + 1])

            def take_v(a, p, r):
                act.wait_ge(ATT[p]["v_mm"], r + 1)
                for q in range(2):
                    for h in range(HK):
                        ins = nc.scalar.activation(vbd_part(p, q, h), v_part(p, q, h), ACT.Copy)
                ins.then_inc(ATT[p]["v_act"], 1)

            def exponentials(a, p, r):
                for u in range(TP):
                    act.wait_ge(ATT[p]["scaled"], r * TP + (u + 1))
                    nc.scalar.activation(sc[:, TP * p + u], sc[:, TP * p + u], ACT.Exp,
                                         scale=[D ** -0.5, HD ** -0.5][a]).then_inc(ATT[p]["prob"], 1)

            def take_pt(a, p, r):
                for u in range(TP):
                    act.wait_ge(ATT[p]["pt_mm"], r * TP + (u + 1))
                    nc.scalar.activation(pT[:, TP * p + u].rearrange("p c q -> p (c q)"), bank(TP * p + u, True)[:, 0:KC * P],
                                         ACT.Copy).then_inc(ATT[p]["pt_ev"], 1)

            def take_at(a, p, r):
                act.wait_ge(ATT[p]["at_mm"], r + 1)
                src = banks(p, True)[0:FC, :, 0:NC_ * P].rearrange("p t (c q) -> p t c q", c=NC_)
                ins = nc.scalar.activation(aT[0:FC, tiles(p)], src, ACT.Copy)
                ins.then_inc(ATT[p]["at_ev"], 1)

            def take_ln(a, p, r):
                act.wait_ge(ATT[p]["ln_mm"], r + 1)
                src = banks(p, True)[0:FC, :, 0:NC_ * P].rearrange("p t (c q) -> p t c q", c=NC_)
                for c in range(NC_):
                    ins = nc.scalar.activation(lnT[0:FC, c, tiles(p)], src[:, :, c], ACT.Identity,
                                               scale=col[:, 2 * a, c:c + 1], bias=col[:, 2 * a + 1, c:c + 1])
                ins.then_inc(ATT[p]["ln_ev"], 1)

            def second_best(p, g):
                act.wait_ge(TOK[p]["dif"], g + 1)
                nc.scalar.activation(exd[:, tiles(p)], dif[:, tiles(p)], ACT.Exp).then_inc(TOK[p]["exd"], 1)

            stages = {"tok": take_h, "turn": take_turned, "gate": second_best}
            att_stages = {"qk": take_qk, "v": take_v, "score": exponentials, "pt": take_pt, "at": take_at, "ln": take_ln}
            with act.Fori(0, G) as g:
                for stage, p in ORDER:
                    if stage in stages:
                        stages[stage](p, g)
                    elif stage[:-1] in att_stages:
                        att_stages[stage[:-1]](int(stage[-1]), p, g * 2 + int(stage[-1]))

            def turn(i, b):
                act.wait_ge(s_xgfree, i + 1)
                for c in range(NC_):
                    ins = nc.scalar.activation(xgT[0:FC, b, c], ps[0:FC, b, c * P:(c + 1) * P], ACT.Identity,
                                               scale=col[:, 2, c:c + 1], bias=col[:, 3, c:c + 1])
                ins.then_inc(s_xgT, 1)

            def gelu(i, b):
                act.wait_ge(s_up, i + 1)
                for u in range(2):
                    ins = nc.scalar.activation(hid[:, b, u * 3:u * 3 + 3].rearrange("p m q -> p (m q)"),
                                               ps[:, 2 + 2 * b + u, 0:3 * P], ACT.Gelu)
                ins.then_inc(s_hid, 1)

            nc.scalar.activation(warm_act[:], minus_half[:, 0:1], ACT.Gelu)
            turn(0, 0)
            turn(1, 1)
            gelu(0, 0)
            with act.Fori(0, (BLOCKS - 3) // 2) as j:
                for k in range(2):
                    gelu(2 * j + (k + 1), 1 - k)
                    turn(2 * j + (k + 2), k)
            gelu(BLOCKS - 2, 1)
            turn(BLOCKS - 1, 0)
            gelu(BLOCKS - 1, 0)
            act.wait_ge(s_add, 16 * BLOCKS)
            for u in range(1, LQ, 2):
                act.dma_start(part(fs, u), part_rows(acc, u)).then_inc(s_fs[u], 16)
            for u in range(LQ):
                n = (u + 1) * HN - 1
                act.wait_ge(s_off, u + 1)
                nc.scalar.activation(fo[:, n], fs[:, n], ACT.Identity, scale=frs[:, n:n + 1], bias=off[:, u:u + 1]
                                     ).then_inc(s_fin_a, 1)

        @block.vector
        def _(dve):
            s0 = Steps(dve, s_dve0)
            nc.vector.memset(ones[:], 1.0).then_inc(s_ones, 1)
            s0.done(nc.vector.memset(wqkv1[:], 0.0))
            s0.join()
            nc.vector.tensor_copy(wqkv1[0:1, 0, 0, 0:1], wqkv1[0:1, 0, 0, 0:1]).then_inc(s_bd_zero, 1)
            s0.done(nc.vector.memset(empty[:], 0.0))
            s0.done(nc.vector.memset(big2[:], 0.0))
            nc.vector.memset(run[:], 0.0).then_inc(s_run, 1)
            s0.done(nc.vector.memset(lnT[FC:FC + 1], 1.0))
            s0.done(nc.vector.memset(aT[FC:FC + 1], 1.0))
            dve.wait_ge(s_const, 16)
            s0.join()
            nc.vector.tensor_copy(empty[:, RW - 1:RW].bitcast(I32), cst[:, C_TOK + TG:C_END]).then_inc(s_zero_tile, 1)
            s0.done(nc.vector.tensor_copy(toks[:], cst[:, C_TOK:C_TOK + TG]))
            s0.done(nc.vector.tensor_copy(upper[:], cst[:, C_U:C_U + P]))
            s0.done(nc.vector.tensor_copy(mask_q[:], cst[0:FC, C_MQ:C_MQ + P]))
            s0.done(nc.vector.tensor_copy(mask_k[:], cst[0:FC, C_MK:C_MK + H * QT]))
            s0.done(nc.vector.tensor_scalar(base[:], cst[:, C_IO:C_IO + E], float(CAP), None, ALU.mult))
            s0.join()
            s0.done(nc.vector.tensor_copy(pos[:, 0], base[:]))
            s0.join()
            nc.vector.tensor_copy(pos[:, 0], base[:]).then_inc(s_counted, PAIRS)
            dve.wait_ge(s_counted, PAIRS)
            nc.vector.tensor_copy(pos[:, 0], base[:]).then_inc(s_prep, 1)

            def keys(a, p, r, s):
                dve.wait_ge(ATT[p]["k_ev"], r + 1)
                for h in range(HC - ACT_HEADS):
                    ins = nc.vector.tensor_scalar(kbd[:, :, h, tokens(p)], kT[:, :, tokens(p)], hmask[0:FC, h:h + 1],
                                                  None, ALU.mult)
                ins.then_inc(ATT[p]["kbd"], 1)

            def values(a, p, r, s):
                dve.wait_ge(ATT[p]["v_mm"], r + 1)
                for q in range(2, 4):
                    for h in range(HK):
                        ins = nc.vector.tensor_copy(vbd_part(p, q, h), v_part(p, q, h))
                ins.then_inc(ATT[p]["v_dve"], 1)

            def maxima(a, p, r, s):
                for u in range(TP):
                    t = TP * p + u
                    score = bank(t)[:, 0:H * QT].rearrange("p (h k) -> p h k", h=H)
                    dve.wait_ge(ATT[p]["score"], r * TP + (u + 1))
                    s.done(nc.vector.tensor_reduce(mx[:, t], score, AX_X, ALU.max))
                    s.join()
                    nc.vector.tensor_tensor(sc[:, t], score, mx[:, t].unsqueeze(2).broadcast_to([P, H, QT]),
                                            ALU.subtract).then_inc(ATT[p]["scaled"], 1)

            def sums(a, p, r, s):
                dve.wait_ge(ATT[p]["prob"], (r + 1) * TP)
                s.done(nc.vector.tensor_reduce(sm[:, tiles(p)], sc[:, tiles(p)], AX_X, ALU.add))
                s.join()
                s.done(nc.vector.reciprocal(ri[:, tiles(p)], sm[:, tiles(p)]))

            def normalised(a, p, r, s):
                s.join()
                for u in range(TP):
                    t = TP * p + u
                    dve.wait_ge(ATT[p]["av"], r * TP + (u + 1))
                    nc.vector.tensor_tensor(at[:, t].rearrange("p (h d) -> p h d", h=H),
                                            bank(t)[:, 0:D].rearrange("p (h d) -> p h d", h=H),
                                            ri[:, t].unsqueeze(2).broadcast_to([P, H, HD]), ALU.mult
                                            ).then_inc(ATT[p]["at"], 1)

            def residual(a, p, r, s):
                S, pt = ATT[p], tiles(p)
                for u in range(TP):
                    t = TP * p + u
                    dve.wait_ge(S["proj"], r * TP + (u + 1))
                    s.done(nc.vector.tensor_tensor(rs[:, t], bank(t)[:, 0:D], hs[:, t], ALU.add))
                    s.join()
                    s.done(nc.vector.bn_stats(st[:, t], rs[:, t]))
                    s.join()
                    s.done(nc.vector.bn_aggr(mv[:, t], st[:, t]))
                s.join()
                var = mv[:, pt, 1]
                add = nc.vector.tensor_scalar(ve[:, p, 0], var, EPS, None, ALU.add)
                if a == 0:
                    s.done(add)
                    s.join()
                    s.done(nc.vector.reciprocal(both[:, p], ve[:, p, 0]))
                    s.join()
                    s.done(nc.vector.tensor_tensor(both[:, p], both[:, p], var, ALU.mult))
                    s.join()
                    nc.vector.tensor_scalar(ve[:, p, 1], both[:, p], EPS, None, ALU.add).then_inc(S["var"], 1)
                else:
                    add.then_inc(S["var"], 1)

            def normalise(a, p, r, s, g):
                S, pt = ATT[p], tiles(p)
                if a == 0:
                    dve.wait_ge(S["rstd"], r + 1)
                    s.done(nc.vector.tensor_tensor(both[:, p], rstd[:, p, 0], rstd[:, p, 1], ALU.mult))
                    s.join()
                    for u in range(TP):
                        t = TP * p + u
                        nc.vector.tensor_scalar(xh[:, t], rs[:, t], mv[:, t, 0:1], both[:, p, u:u + 1], ALU.subtract,
                                                ALU.mult).then_inc(S["res"], 1)
                    for u in range(TP):
                        t = TP * p + u
                        s.done(nc.vector.tensor_scalar(hs[:, t], rs[:, t], mv[:, t, 0:1], rstd[:, p, 0, u:u + 1],
                                                       ALU.subtract, ALU.mult))
                else:
                    nc.vector.tensor_tensor(xr[:, bass.ds(g * TG + TP * p, TP)], rs[:, pt], hs[:, pt], ALU.add
                                            ).then_inc(s_xr, 1)
                    dve.wait_ge(s_left, g + 1)
                    dve.wait_ge(S["rstd"], r + 1)
                    for u in range(TP):
                        t = TP * p + u
                        nc.vector.tensor_scalar(xd[:, t, 0:D], rs[:, t], mv[:, t, 0:1], rstd[:, p, 0, u:u + 1], ALU.subtract,
                                                ALU.mult).then_inc(S["res"], 1)

            def choose(p, g, s):
                pt = tiles(p)
                dve.wait_ge(TOK[p]["gate"], g + 1)
                s.done(nc.vector.tensor_copy(lg[:, pt], banks(p)[:, :, 0:E]))
                s.join()
                for u in range(TP):
                    s.done(nc.vector.max(top[:, TP * p + u], lg[:, TP * p + u]))
                s.join()
                for u in range(TP):
                    s.done(nc.vector.max_index(tix[:, TP * p + u], top[:, TP * p + u], lg[:, TP * p + u]))
                nc.vector.tensor_tensor(dif[:, pt], top[:, pt, 1:2], top[:, pt, 0:1], ALU.subtract).then_inc(TOK[p]["dif"], 1)
                s.join()
                s.done(nc.vector.tensor_copy(tixf[:, pt], tix[:, pt, 0:2]))
                s.join()
                s.done(nc.vector.tensor_tensor(hot[:, pt].rearrange("p t k e -> p (t k) e"),
                                               cst[:, C_IO:C_IO + E].unsqueeze(1).broadcast_to([P, 2 * TP, E]),
                                               tixf[:, pt].rearrange("p t k -> p (t k)").unsqueeze(2).broadcast_to([P, 2 * TP, E]),
                                               ALU.is_equal))
                s.join()
                nc.vector.tensor_tensor(hotb[:, pt], hot[:, pt, 0], hot[:, pt, 1], ALU.add).then_inc(TOK[p]["hot"], 1)

            def place(p, g, s):
                pt = tiles(p)
                dve.wait_ge(TOK[p]["exd"], g + 1)
                s.done(nc.vector.tensor_scalar(den[:, pt], exd[:, pt], 1.0, None, ALU.add))
                s.join()
                s.done(nc.vector.reciprocal(w01[:, pt, 0:1], den[:, pt]))
                s.join()
                s.done(nc.vector.tensor_tensor(w01[:, pt, 1:2], w01[:, pt, 0:1], exd[:, pt], ALU.mult))
                s.join()
                s.done(nc.vector.tensor_tensor(hw[:, pt], hot[:, pt], w01[:, pt].unsqueeze(3).broadcast_to([P, TP, 2, E]),
                                               ALU.mult))
                s.join()
                s.done(nc.vector.tensor_tensor(xd[:, pt, D:D + E], hw[:, pt, 0], hw[:, pt, 1], ALU.add))
                s.done(nc.vector.tensor_copy(xd[:, pt, RW - 1:RW].bitcast(I32), toks[:, pt].unsqueeze(2)))
                s.join()
                s.done(nc.vector.tensor_scalar(toks[:, pt], toks[:, pt], float(TG * P), None, ALU.add))
                dve.wait_ge(TOK[p]["rank"], g + 1)
                s.done(nc.vector.tensor_tensor(run[:], run[:], hotb[:, TP * p], ALU.add))
                nc.vector.tensor_tensor(pos[:, pt], banks(p, True)[:, :, 0:E], base[:].unsqueeze(1).broadcast_to([P, TP, E]),
                                        ALU.add).then_inc(s_counted, 1)
                dve.wait_ge(s_counted, g * PAIRS + (PAIRS + p + 1))
                s.done(nc.vector.tensor_tensor(pick[:, pt], hot[:, pt],
                                               pos[:, pt].unsqueeze(2).broadcast_to([P, TP, 2, E]), ALU.mult))
                s.join()
                s.done(nc.vector.tensor_reduce(slf[:, pt], pick[:, pt], AX_X, ALU.add))
                nc.vector.tensor_tensor(run[:], run[:], hotb[:, TP * p + 1], ALU.add).then_inc(s_run, 1)
                s.join()
                nc.vector.tensor_copy(slot_v[:, pt], slf[:, pt]).then_inc(TOK[p]["slot"], 1)

            stages = {"gate": choose, "rank": place}
            att_stages = {"qk": keys, "v": values, "score": maxima, "pt": sums, "av": normalised, "proj": residual, "norm": normalise}
            with dve.Fori(0, G) as g:
                s = Steps(dve, s_dve)
                for stage, p in ORDER:
                    if stage in stages:
                        stages[stage](p, g, s)
                    elif stage[:-1] in att_stages:
                        more = (g,) if stage[:-1] == "norm" else ()
                        att_stages[stage[:-1]](int(stage[-1]), p, g * 2 + int(stage[-1]), s, *more)
                s.join()
                dve.sem_clear(s_dve)

            s2 = Steps(dve, s_dve2)
            io = cst[:, C_IO:C_IO + E]
            iob = cst[:, C_IO:C_IO + BLOCKS]
            dve.wait_ge(s_cnt, 1)
            s2.done(nc.vector.tensor_copy(cnt[:], ps[:, 2, 0:E]))
            s2.done(nc.vector.tensor_scalar(nblk[:], io, float(P), None, ALU.mult))
            s2.join()
            s2.done(nc.vector.tensor_tensor(cmpb[:], cnt[:].unsqueeze(2).broadcast_to([P, E, E]),
                                            nblk[:].unsqueeze(1).broadcast_to([P, E, E]), ALU.is_gt))
            s2.join()
            s2.done(nc.vector.tensor_reduce(nblk[:], cmpb[:], AX_X, ALU.add))
            s2.join()
            s2.done(nc.vector.tensor_copy(lastb[:], nblk[:]))
            for e in range(1, E):
                s2.join()
                s2.done(nc.vector.tensor_tensor(lastb[:, e:e + 1], lastb[:, e - 1:e], lastb[:, e:e + 1], ALU.add))
            s2.join()
            iob_e = iob.unsqueeze(2).broadcast_to([P, BLOCKS, E])
            last_e = lastb[:].unsqueeze(1).broadcast_to([P, BLOCKS, E])
            s2.done(nc.vector.tensor_tensor(cmp2[:], last_e, iob_e, ALU.is_le))
            s2.join()
            s2.done(nc.vector.tensor_reduce(eof[:], cmp2[:], AX_X, ALU.add))
            s2.done(nc.vector.tensor_tensor(cmp3[:], cmp2[:], nblk[:].unsqueeze(1).broadcast_to([P, BLOCKS, E]), ALU.mult))
            s2.join()
            s2.done(nc.vector.tensor_reduce(fst[:], cmp3[:], AX_X, ALU.add))
            s2.done(nc.vector.tensor_scalar(rowf[:], eof[:], float(CAP // P), None, ALU.mult))
            s2.join()
            s2.done(nc.vector.tensor_tensor(fst[:], iob, fst[:], ALU.subtract))
            s2.join()
            s2.done(nc.vector.tensor_tensor(rowf[:], rowf[:], fst[:], ALU.add))
            s2.done(nc.vector.tensor_scalar(tab_e[:], eof[:], float(E - 1), None, ALU.min))
            s2.done(nc.vector.memset(xgT[FC:FC + 1], 1.0))
            s2.join()
            nc.vector.tensor_scalar(tab_row[:], rowf[:], float(P), float(E * CAP), ALU.mult, ALU.min).then_inc(s_tab, 1)
            dve.wait_ge(s_tab, 1)
            dve.wait_ge(s_moew, 16 * (1 + 3 * E))

            def expert(i):
                return dve.value_load(tab_e[0:1, bass.ds(i, 1)], min_val=0, max_val=E - 1)

            def stage_w1(i, b):
                e = expert(i)
                nc.vector.tensor_copy(w1c[0:FC, b, 0], w1s[0:FC, bass.ds(e, 1), 0].rearrange("p o n -> p (o n)"))
                nc.vector.tensor_copy(w1c[:, b, 1], w1s[:, bass.ds(e, 1), 1].rearrange("p o n -> p (o n)")
                                      ).then_inc(s_w1c, 1)

            def take_y(i, b, xb, k, first=False):
                e = expert(i)
                dve.wait_ge(s_down, i + 1)
                if not first:
                    dve.wait_ge(s_add, 16 * (i - 1))
                nc.vector.tensor_tensor(yb[:, b], ps[:, 6 + b, 0:D], b2s[:, bass.ds(e, 1)].rearrange("p o n -> p (o n)"),
                                        ALU.add).then_inc(s_dve4, 1)
                dve.wait_ge(s_dve4, k)
                nc.vector.tensor_tensor(yb[:, b], yb[:, b], xg[:, xb, bass.ds(e + D, 1)].broadcast_to([P, D]),
                                        ALU.mult).then_inc(s_y, 1)

            stage_w1(0, 0)
            stage_w1(1, 1)
            for i in range(XB):
                dve.wait_ge(s_up, i + 1)
                stage_w1(i + 2, i % 2)
                take_y(i, i % 2, i, i + 1, first=i < 2)
            dve.sem_clear(s_dve4)
            with dve.Fori(1, BLOCKS // XB) as j:
                for b in range(XB):
                    dve.wait_ge(s_up, XB * j + (b + 1))
                    stage_w1(XB * j + b + 2, b % 2)
                    take_y(XB * j + b, b % 2, b, b + 1)
                dve.sem_clear(s_dve4)
            for i in range(BLOCKS // XB * XB, BLOCKS):
                if i + 2 < BLOCKS:
                    dve.wait_ge(s_up, i + 1)
                    stage_w1(i + 2, i % 2)
                take_y(i, i % 2, i % XB, i % XB + 1)

            s3 = Steps(dve, s_dve3)

            def statistics(u):
                dve.wait_ge(s_fs[u], 16)
                for n in range(u * HN, (u + 1) * HN):
                    s3.done(nc.vector.bn_stats(fst6[:, n], fs[:, n]))
                s3.join()
                for n in range(u * HN, (u + 1) * HN):
                    s3.done(nc.vector.bn_aggr(fmv[:, n], fst6[:, n]))
                s3.join()
                nc.vector.tensor_scalar(part(fve, u), part(fmv, u)[:, :, 1], EPS, None, ALU.add).then_inc(s_fvar, 1)

            def finish(u):
                n = (u + 1) * HN - 1
                dve.wait_ge(s_frs, u + 1)
                nc.vector.tensor_scalar(off[:, u:u + 1], fmv[:, n, 0:1], frs[:, n:n + 1], -1.0, ALU.mult, ALU.mult
                                        ).then_inc(s_off, 1)
                for n in range(u * HN, (u + 1) * HN - 1):
                    ins = nc.vector.tensor_scalar(fo[:, n], fs[:, n], fmv[:, n, 0:1], frs[:, n:n + 1], ALU.subtract, ALU.mult)
                ins.then_inc(s_fin, 1)

            statistics(0)
            for u in range(1, LQ):
                statistics(u)
                finish(u - 1)
            finish(LQ - 1)

        @block.tensor
        def _(pe):
            mm = nc.tensor.matmul
            tr = nc.tensor.transpose

            def keep_warm(n):
                for i in range(n):
                    mm(bank(0, True)[:, 0:P], ones[:], ones[:], start=True, stop=True)

            pe.wait_ge(s_ones, 1)
            keep_warm(30)
            pe.wait_ge(s_wtok, 32)

            def embed(p, g):
                for u in range(TP):
                    t = TP * p + u
                    pe.wait_ge(s_x[t], (g + 1) * 16 + (16 if t == 0 else 0))
                    for k in range(KIN):
                        ins = mm(bank(t)[:, 0:D], xin[:, t, k], wtok[:, k], start=(k == 0), stop=(k == KIN - 1))
                    ins.then_inc(TOK[p]["tok"], 1)

            def turn_tile(t, src):
                for c in range(NC_):
                    ins = tr(bank(t, True)[0:FC, c * P:(c + 1) * P], src[:, t, c * FC:(c + 1) * FC], ident)
                return ins

            def turn_h(p, g):
                if p == 0:
                    pe.wait_ge(s_prep, 1)
                pe.wait_ge(TOK[p]["h"], g + 1)
                pe.wait_ge(s_counted, g * PAIRS + (p + 1))
                for t in range(TP * p, TP * p + TP):
                    ins = turn_tile(t, hs)
                ins.then_inc(TOK[p]["hT"], 1)

            def keys_queries(a, p, r, g):
                S = ATT[p]
                if a == 0:
                    pe.wait_ge(s_wq1, 16 * (H + 1))
                    pe.wait_ge(TOK[p]["lnT"], g + 1)
                else:
                    pe.wait_ge(ATT[p]["ln_ev"], r)
                for b, kind, name in ((0, 1, "k_mm"), (1, 0, "q_mm")):
                    for c in range(NC_):
                        dst = bank(TP * p + b)[0:FC, c * TP * P:(c + 1) * TP * P]
                        if a == 0:
                            ins = mm(dst, wqkv1[:, c, kind], lnT[:, c, tiles(p)].rearrange("p t q -> p (t q)"),
                                     start=True, stop=True)
                        else:
                            for k in range(NC_):
                                ins = mm(dst, wqkv2[:, k, kind * D + c * FC:kind * D + (c + 1) * FC],
                                         lnT[0:FC, k, tiles(p)].rearrange("p t q -> p (t q)"),
                                         start=(k == 0), stop=(k == NC_ - 1))
                    ins.then_inc(S[name], 1)

            def values(a, p, r):
                for t in range(TP * p, TP * p + TP):
                    for c in range(NC_):
                        if a == 0:
                            ins = mm(bank(t, True)[:, c * FC:(c + 1) * FC], lnT[:, c, t], wqkv1[:, c, 2], start=True, stop=True)
                        else:
                            ins = mm(bank(t, True)[:, 0:D], lnT[0:FC, c, t], wqkv2[:, c, 2 * D:3 * D],
                                     start=(c == 0), stop=(c == NC_ - 1))
                ins.then_inc(ATT[p]["v_mm"], 1)

            def scores(a, p, r):
                S = ATT[p]
                pe.wait_ge(S["q_ev"], r + 1)
                pe.wait_ge(S["kbd"], r + 1)
                for t in range(TP * p, TP * p + TP):
                    mm(bank(t)[:, 0:H * QT], mask_q[:], mask_k[:], start=True, stop=False, skip_group_check=True)
                    for c in range(NC_):
                        for q in range(4):
                            tok = slice(t * P + q * QT, t * P + (q + 1) * QT)
                            ins = mm(bank(t)[q * QT:(q + 1) * QT, c * HC * QT:(c + 1) * HC * QT], qT[:, c, tok],
                                     kbd[:, c, :, tok], start=False, stop=(c == NC_ - 1), skip_group_check=True)
                    ins.then_inc(S["score"], 1)

            def turn_probs(a, p, r):
                S = ATT[p]
                pe.wait_ge(S["v_act"], r + 1)
                pe.wait_ge(S["v_dve"], r + 1)
                for u in range(TP):
                    t = TP * p + u
                    pe.wait_ge(S["prob"], r * TP + (u + 1))
                    for c in range(KC):
                        ins = tr(bank(t, True)[:, c * P:(c + 1) * P],
                                 sc[:, t].rearrange("p h k -> p (h k)")[:, c * P:(c + 1) * P], ident)
                    ins.then_inc(S["pt_mm"], 1)

            def attend(a, p, r):
                S = ATT[p]
                for u in range(TP):
                    t = TP * p + u
                    pe.wait_ge(S["pt_ev"], r * TP + (u + 1))
                    for c in range(KC):
                        for q in range(4):
                            ins = mm(bank(t)[q * QT:(q + 1) * QT, c * HK * HD:(c + 1) * HK * HD],
                                     pT[:, t, c, q * QT:(q + 1) * QT], vbd[:, t, q, c], start=True, stop=True)
                    ins.then_inc(S["av"], 1)

            def turn_attended(a, p, r):
                for u in range(TP):
                    pe.wait_ge(ATT[p]["at"], r * TP + (u + 1))
                    ins = turn_tile(TP * p + u, at)
                ins.then_inc(ATT[p]["at_mm"], 1)

            def project(a, p, r):
                pe.wait_ge(s_w2nd, 16 * 7)
                pe.wait_ge(ATT[p]["at_ev"], r + 1)
                for t in range(TP * p, TP * p + TP):
                    for c in range(NC_):
                        K = FC + (c == NC_ - 1)
                        ins = mm(bank(t)[:, 0:D], aT[0:K, t, c], wout[a][0:K, c], start=(c == 0), stop=(c == NC_ - 1))
                    ins.then_inc(ATT[p]["proj"], 1)

            def turn_ln(a, p, r):
                for u in range(TP):
                    pe.wait_ge(ATT[p]["res"], r * TP + (u + 1))
                    ins = turn_tile(TP * p + u, (xh, xd)[a])
                ins.then_inc(ATT[p]["ln_mm"], 1)

            def gates(p, g):
                pe.wait_ge(ATT[p]["ln_ev"], g * 2 + 2)
                for t in range(TP * p, TP * p + TP):
                    for c in range(NC_):
                        K = FC + (c == NC_ - 1)
                        ins = mm(bank(t)[:, 0:E], lnT[0:K, c, t], wgate[0:K, c], start=(c == 0), stop=(c == NC_ - 1))
                ins.then_inc(TOK[p]["gate"], 1)

            def count(p, g):
                pe.wait_ge(TOK[p]["hot"], g + 1)
                pe.wait_ge(s_run, g * PAIRS + (p + 1))
                for u in range(TP):
                    dst = bank(TP * p + u, True)[:, 0:E]
                    mm(dst, upper[:], hotb[:, TP * p + u], start=True, stop=False)
                    if u:
                        mm(dst, ones[:], hotb[:, TP * p], start=False, stop=False)
                    ins = mm(dst, ones[:], run[:], start=False, stop=True)
                ins.then_inc(TOK[p]["rank"], 1)

            stages = {"tok": embed, "turn": turn_h, "gate": gates, "rank": count}
            att_stages = {"qk": keys_queries, "v": values, "score": scores, "pt": turn_probs, "av": attend,
                          "at": turn_attended, "proj": project, "ln": turn_ln}
            with pe.Fori(0, G) as g:
                for stage, p in ORDER:
                    if stage in stages:
                        stages[stage](p, g)
                    elif stage[:-1] in att_stages:
                        more = (g,) if stage[:-1] == "qk" else ()
                        att_stages[stage[:-1]](int(stage[-1]), p, g * 2 + int(stage[-1]), *more)
            pe.wait_ge(s_run, G * PAIRS + 1)
            mm(ps[:, 2, 0:E], ones[:], run[:], start=True, stop=True).then_inc(s_cnt, 1)

            pe.wait_ge(s_tab, 1)
            pe.wait_ge(s_moew, 16 * (1 + 3 * E))
            keep_warm(70)

            def turn_rows(b, xb, j):
                pe.wait_ge(s_xg[xb], 16 * (j + 1))
                for c in range(NC_):
                    ins = tr(ps[0:FC, b, c * P:(c + 1) * P], xg[:, xb, c * FC:(c + 1) * FC], ident)
                ins.then_inc(s_xgfree, 1)

            def up(i, b):
                pe.wait_ge(s_w1c, i + 1)
                pe.wait_ge(s_xgT, i + 1)
                for m in range(MH):
                    for c in range(NC_):
                        K = FC + (c == NC_ - 1)
                        ins = mm(ps[:, 2 + 2 * b + m // 3, m % 3 * P:(m % 3 + 1) * P], w1c[0:K, b, c, m * P:(m + 1) * P],
                                 xgT[0:K, b, c], start=(c == 0), stop=(c == NC_ - 1))
                ins.then_inc(s_up, 1)

            def down(i, b):
                e = pe.value_load(tab_e[0:1, bass.ds(i, 1)], min_val=0, max_val=E - 1)
                pe.wait_ge(s_hid, i + 1)
                for m in range(MH):
                    ins = mm(ps[:, 6 + b, 0:D], hid[:, b, m], w2s[:, bass.ds(e, 1), m].rearrange("p o n -> p (o n)"),
                             start=(m == 0), stop=(m == MH - 1))
                ins.then_inc(s_down, 1)

            turn_rows(0, 0, 0)
            turn_rows(1, 1, 0)
            up(0, 0)
            with pe.Fori(0, (BLOCKS - 3) // XB) as j:
                for b in range(XB):
                    i = XB * j + b
                    up(i + 1, 1 - b % 2)
                    turn_rows(b % 2, (b + 2) % XB, j + (b + 2) // XB)
                    down(i, b % 2)
            for i in range((BLOCKS - 3) // XB * XB, BLOCKS - 1):
                up(i + 1, (i + 1) % 2)
                if i + 2 < BLOCKS:
                    turn_rows(i % 2, (i + 2) % XB, (i + 2) // XB)
                if i == BLOCKS - 2:
                    pe.wait_ge(s_y, BLOCKS - 3)
                down(i, i % 2)
            pe.wait_ge(s_y, BLOCKS - 2)
            down(BLOCKS - 1, 0)


def kernel(x, L0_tok_W, L0_attn_W_qkv, L0_attn_b_qkv, L0_attn_W_out, L0_attn_b_out, L0_ffn_ln1_g, L0_ffn_ln1_b,
           L0_ffn_qkv_w, L0_ffn_proj_w, L0_ffn_proj_b, L0_ffn_ln2_g, L0_ffn_ln2_b, L0_ffn_gate_w, L0_ffn_gate_b,
           L0_ffn_w1, L0_ffn_b1, L0_ffn_w2, L0_ffn_b2):
    import concourse.bacc as bacc
    from concourse.bass_utils import run_bass_kernel_spmd

    def laid(a):
        return np.ascontiguousarray(a)

    def chunks(w):
        return laid(np.asarray(w).reshape(NC_, FC, -1).transpose(1, 0, 2))

    n_img, side, p = x.shape[0], x.shape[2] // 16, 16
    patches = np.asarray(x).reshape(n_img, 3, side, p, side, p).transpose(0, 2, 4, 3, 5, 1)
    patches = patches.reshape(NT, P, KIN, P).transpose(0, 3, 2, 1)
    b_qkv = np.asarray(L0_attn_b_qkv).reshape(H, 3, HD).transpose(1, 0, 2).reshape(1, 3, NC_, FC).transpose(0, 2, 1, 3)
    lns = [np.asarray(v).reshape(1, NC_, FC) for v in (L0_ffn_ln1_g, L0_ffn_ln1_b, L0_ffn_ln2_g, L0_ffn_ln2_b)]
    arrays = {
        "consts": constants(),
        "patches": laid(patches),
        "w_tok": laid(np.asarray(L0_tok_W).T.reshape(KIN, P, D).transpose(1, 0, 2)),
        "w_qkv1": laid(L0_attn_W_qkv),
        "b_qkv1": laid(b_qkv),
        "ln_gb": laid(np.concatenate(lns).transpose(2, 0, 1)),
        "w_out1": chunks(L0_attn_W_out),
        "b_out1": laid(np.asarray(L0_attn_b_out).reshape(1, D)),
        "w_qkv2": chunks(np.asarray(L0_ffn_qkv_w).T),
        "w_proj": chunks(np.asarray(L0_ffn_proj_w).T),
        "b_proj": laid(np.asarray(L0_ffn_proj_b).reshape(1, D)),
        "gate": chunks(np.asarray(L0_ffn_gate_w).T),
        "gate_b": laid(np.asarray(L0_ffn_gate_b).reshape(1, E)),
        "w1": laid(np.asarray(L0_ffn_w1).transpose(2, 0, 1).reshape(NC_, FC, E, HID).transpose(1, 2, 0, 3)),
        "b1": laid(L0_ffn_b1),
        "w2": laid(np.asarray(L0_ffn_w2).transpose(2, 0, 1).reshape(MH, P, E, D).transpose(1, 2, 0, 3)),
        "b2": laid(L0_ffn_b2),
    }
    nc = bacc.Bacc("TRN2", target_bir_lowering=False, num_devices=1)
    args = [nc.dram_tensor(k, a.shape, mybir.dt.from_np(a.dtype), kind="ExternalInput").ap() for k, a in arrays.items()]
    out = nc.dram_tensor("out", (T, D), F32, kind="ExternalOutput").ap()
    vit_block(nc, *args, out)
    got = run_bass_kernel_spmd(nc, [arrays], core_ids=[0]).results[0]["out"]
    return got.reshape(n_img, side * side, D)
```

```python
from contextlib import ExitStack

import numpy as np
import concourse.bass as bass
from concourse import mybir

ALU = mybir.AluOpType
ACT = mybir.ActivationFunctionType
AX_X = mybir.AxisListType.X
F32 = mybir.dt.float32
BF16 = mybir.dt.bfloat16
I32 = mybir.dt.int32
U32 = mybir.dt.uint32

P = 128
D = 192
T = 1024
NT = T // P
TG = 4
G = NT // TG
H, HD, N_IMG = 12, 16, 16
FC, NC_ = 96, 2
HC = FC // HD
ACT_HEADS = 2
ACT_QUADS = 2
VW = HD + 1
QT = 32
KC = 3
HK = 4
KIN = 768 // P
E, HID = 8, 768
MH = HID // P
CAP = T
RW = D + E + 1
XB = 4
BLOCKS = (2 * T + E * (P - 1)) // P
LQ = 4
HN = NT // LQ
EPS = 1e-5
NEG = -1e30

ORDER = [(stage[:-1], "ABCD".index(stage[-1])) for stage in (
    "tokA tokB turnA tokC turnB qk0A turnC qk0B v0A qk0C s0A tokD v0B s0B pt0A turnD v0C s0C pt0B av0A qk0D "
    "pt0C av0B at0A v0D s0D proj0A av0C at0B pt0D norm0A proj0B at0C av0D norm0B ln0A proj0C at0D ln0B qk1A "
    "norm0C proj0D qk1B ln0C norm0D v1A s1A v1B ln0D s1B qk1C pt1A qk1D v1C av1A pt1B v1D s1D at1A s1C av1B "
    "pt1D proj1A at1B pt1C av1D norm1A proj1B av1C at1D norm1B ln1A proj1D at1C ln1B proj1C norm1D gateB ln1D "
    "norm1C ln1C rankB gateD rankD").split()]


def nth(stage, t, g=0, both=True):
    def kind(s):
        return s.rstrip("01") if both else s

    same = [s for s in ORDER if kind(s[0]) == kind(stage)]
    return g * len(same) + (same.index((stage, t)) + 1)


def later(stage, t):
    return max((t - 1, t), key=lambda u: nth(stage, u))


C_ID, C_U, C_HM, C_IO, C_TOK, C_END = np.cumsum([0, P, P, HC, BLOCKS + 1, TG + 1]).tolist()


def constants():
    c = np.zeros((P, C_END), np.float32)
    tok = np.arange(P)
    c[:, C_ID:C_ID + P] = np.eye(P)
    c[:, C_U:C_U + P] = tok[:, None] < tok[None, :]
    for h in range(HC):
        c[h * HD:(h + 1) * HD, C_HM + h] = 1.0
    c[:, C_IO:C_TOK] = np.arange(BLOCKS + 1)
    c[:, C_TOK:C_TOK + TG] = tok[:, None] + P * np.arange(TG)
    c[:, C_TOK + TG] = T + tok
    return c


def image_masks():
    m = np.zeros((2, P + H * QT), np.float32)
    for g in range(2):
        m[g, 0:P] = (np.arange(P) // N_IMG) % 2 == g
        m[g, P:] = np.where((np.arange(H * QT) % QT) // N_IMG == g, 0.0, NEG)
    return m


class Steps:

    def __init__(self, eng, sem, base=0):
        self.eng, self.sem, self.base, self.n = eng, sem, base, 0

    def done(self, ins):
        ins.then_inc(self.sem, 1)
        self.n += 1
        return self.n

    def join(self, n=None):
        self.eng.wait_ge(self.sem, self.base + (self.n if n is None else n))


def vit_block(nc, consts, masks, x, w_tok, w_qkv1, b_qkv1, ln_gb, w_out1, b_out1, w_qkv2, w_proj, b_proj, gate, gate_b,
              w1, b1, w2, b2, out):
    with ExitStack() as ctx:
        def sb(name, shape, dt=F32):
            return ctx.enter_context(nc.sbuf_tensor("sb_" + name, shape, dt))

        def sem(name):
            return ctx.enter_context(nc.semaphore(name))

        ps = ctx.enter_context(nc.psum_tensor("ps", [P, 8, 512], F32))
        rows_in = nc.dram_tensor("rows_in", [E * CAP + P, RW], F32).ap()
        acc = nc.dram_tensor("acc", [T + P, D], F32).ap()

        cst = sb("cst", [P, C_END])
        ident = cst[:, C_ID:C_ID + P]
        hmask = cst[:, C_HM:C_HM + HC]
        upper = sb("upper", [P, P], BF16)
        ones = sb("ones", [P, P], BF16)
        msk = sb("msk", [2, P + H * QT])
        mask_q = sb("mask_q", [FC, P], BF16)
        mask_k = sb("mask_k", [FC, H * QT], BF16)
        minus_half = sb("minus_half", [P, 2])
        wtok = sb("wtok", [P, KIN, D])
        wheads = sb("wheads", [FC, NC_, 3, HD])
        wqkv1 = sb("wqkv1", [FC + 1, NC_, 3, FC])
        wqkv2 = sb("wqkv2", [FC, NC_, 3 * D])
        wout = [sb(f"wout{a}", [FC + 1, NC_, D]) for a in range(2)]
        wgate = sb("wgate", [FC + 1, NC_, E])
        col = sb("col", [FC, 4, NC_])
        b2s = sb("b2s", [P, E, D])
        w1s = sb("w1s", [FC + 1, E, NC_, HID])
        w2s = sb("w2s", [P, E, MH, D])
        tick = sb("tick", [P, 1])
        warm_act = sb("warm_act", [P, 1])
        empty = sb("empty", [P, RW])

        xin = sb("xin", [P, TG, KIN, P])
        hs = sb("hs", [P, TG, D])
        lnT = sb("lnT", [FC + 1, NC_, TG, P])
        aT = sb("aT", [FC + 1, TG, NC_, P])
        qk = sb("qk", [P, 2 * NC_ * TG * P])
        qT, kT = (qk[0:FC, i * NC_ * TG * P:(i + 1) * NC_ * TG * P].rearrange("p (c n) -> p c n", c=NC_) for i in range(2))
        big = sb("big", [P, NC_ * HC * TG * P])
        big2 = sb("big2", [P, TG * 4 * KC * HK * VW])
        kbd = big[0:FC].rearrange("p (c h n) -> p c h n", c=NC_, h=HC)
        vbd = big2[:].rearrange("p (t q c n) -> p t q c n", t=TG, q=4, c=KC)
        sc = sb("sc", [P, TG, H, QT])
        xh = sc[:].rearrange("p t h k -> p t (h k)")[:, :, 0:D]
        pT = sb("pT", [P, TG, KC, P])
        mx = sb("mx", [P, TG, H])
        ri = sb("ri", [P, TG, H])
        at = sb("at", [P, TG, D])
        rs = at
        xd = sb("xd", [P, TG, RW])
        st = sb("st", [P, TG, 6])
        mv = sb("mv", [P, TG, 2])
        ve = sb("ve", [P, TG, 2])
        rstd = sb("rstd", [P, TG, 2])
        lg = sb("lg", [P, TG, E])
        top = sb("top", [P, TG, E])
        tix = sb("tix", [P, TG, E], U32)
        dif = sb("dif", [P, TG, 1])
        exd = sb("exd", [P, TG, 1])
        den = sb("den", [P, TG, 1])
        hot = sb("hot", [P, TG, 2, E])
        hotb = sb("hotb", [P, TG, E], BF16)
        run = sb("run", [P, E], BF16)
        pos = sb("pos", [P, TG, E])
        base = sb("base", [P, E])
        pick = sb("pick", [P, TG, 2, E])
        slot_v = sb("slot_v", [P, TG, 2], I32)
        slot_g = sb("slot_g", [P, TG, 2], I32)
        w01 = sb("w01", [P, TG, 2])
        hw = sb("hw", [P, TG, 2, E])
        toks = sb("toks", [P, TG])
        xr = sb("xr", [P, NT, D])
        cnt = sb("cnt", [P, E])
        cmpb = sb("cmpb", [P, E, E])
        nblk = sb("nblk", [P, E])
        lastb = sb("lastb", [P, E])
        cmp2 = sb("cmp2", [P, BLOCKS, E])
        eof = sb("eof", [P, BLOCKS])
        cmp3 = sb("cmp3", [P, BLOCKS, E])
        fst = sb("fst", [P, BLOCKS])
        rowf = sb("rowf", [P, BLOCKS])
        tab_e = sb("tab_e", [P, BLOCKS], I32)
        tab_row = sb("tab_row", [P, BLOCKS], I32)
        xg = qk[:, 0:XB * RW].rearrange("p (b d) -> p b d", b=XB)
        o = XB * RW
        yb = qk[:, o:o + 2 * D].rearrange("p (b d) -> p b d", b=2)
        o += 2 * D
        xgT = qk[0:FC + 1, o:o + 2 * NC_ * P].rearrange("p (b c q) -> p b c q", b=2, c=NC_)
        tok_g = sb("tok_g", [P, 2, 1], I32)
        w1c = big[0:FC + 1, 0:2 * NC_ * HID].rearrange("p (b c n) -> p b c n", b=2, c=NC_)
        hid = big[:, 2 * NC_ * HID:3 * NC_ * HID].rearrange("p (b m q) -> p b m q", b=2, m=MH)
        fo = big2[:, 0:NT * D].rearrange("p (n d) -> p n d", n=NT)
        fs = big[:, 3 * NC_ * HID:3 * NC_ * HID + NT * D].rearrange("p (n d) -> p n d", n=NT)
        fst6 = sb("fst6", [P, NT, 6])
        fmv = sb("fmv", [P, NT, 2])
        fve = sb("fve", [P, NT])
        frs = sb("frs", [P, NT])
        off = sb("off", [P, NT])

        def sems(names):
            return [sem(n) for n in names.split()]

        s_const, s_masks, s_ln_gb = sems("s_const s_masks s_ln_gb")
        s_wtok, s_wtok_rest, s_wheads, s_wq1, s_wlater, s_wmoe = sems("s_wtok s_wtok_rest s_wheads s_wq1 s_wlater s_wmoe")
        s_x, s_x_rest = [sem(f"s_x{t}") for t in range(TG)], sem("s_x_rest")
        s_ones, s_zero_tile, s_zeroed, s_vbd, s_prep = sems("s_ones s_zero_tile s_zeroed s_vbd s_prep")
        S = {n: sem("s_" + n) for n in (
            "tok h hT lnT k_mm k_ev q_mm q_ev kbd v_mm v_act v_dve score scaled prob pt_mm pt_ev av at at_mm at_ev "
            "proj var rstd res x1_there ln_mm ln_ev gate dif exd hot rank slot").split()}
        s_counted, s_run, s_scat, s_left, s_xr, s_acc = sems("s_counted s_run s_scat s_left s_xr s_acc")
        s_dve, s_pool, s_dve_setup, s_pool_setup, s_tables, s_stats, s_y_biased = sems(
            "s_dve s_pool s_dve_setup s_pool_setup s_tables s_stats s_y_biased")
        s_cnt, s_tab, s_xg, s_xgfree = sem("s_cnt"), sem("s_tab"), [sem(f"s_xg{b}") for b in range(XB)], sem("s_xgfree")
        s_xgT, s_w1c, s_up, s_hid, s_down, s_y, s_tok_g, s_add = sems("s_xgT s_w1c s_up s_hid s_down s_y s_tok_g s_add")
        s_fs = [sem(f"s_fs{u}") for u in range(LQ)]
        s_fvar, s_frs, s_off, s_fin, s_fin_a, s_out = sems("s_fvar s_frs s_off s_fin s_fin_a s_out")

        block = ctx.enter_context(nc.Block())

        def bank(t, second=False):
            return ps[:, TG * second + t, :]

        def v_part(t, q, h):
            return bank(t, True)[QT * q:QT * q + QT, 0:D].rearrange("p (c n) -> p c n", c=KC)[:, :, HD * h:HD * h + HD]

        def vbd_part(t, q, h):
            return vbd[QT * h:QT * h + QT, t, q, :, VW * h:VW * h + HD]

        def xr_before(t, g):
            return nth("norm1", t, g, both=False)

        def tokens(t):
            return slice(t * P, (t + 1) * P)

        def part(tile, u):
            return tile[:, u * HN:(u + 1) * HN]

        def part_rows(rows, u):
            return rows[u * HN * P:(u + 1) * HN * P].rearrange("(n p) d -> p n d", p=P)

        @block.sync
        def _(sp):
            def load_x(t, n):
                sp.dma_start(xin[:, t], x[n]).then_inc(s_x[t], 16)

            halves = [slice(k, k + KIN // 2) for k in (0, KIN // 2)]
            for u, half in enumerate(halves):
                sp.dma_start(wtok[:, half], w_tok[:, half]).then_inc((s_wtok, s_wtok_rest)[u], 16)
                sp.dma_start(xin[:, 0, half], x[0, :, half]).then_inc((s_x[0], s_x_rest)[u], 16)
            sp.dma_start(cst[:], consts).then_inc(s_const, 16)
            for t in range(1, TG):
                load_x(t, t)
            sp.dma_start(col[:], ln_gb).then_inc(s_ln_gb, 16)
            for src, bias, dst in ((w_out1, b_out1, wout[0]), (w_proj, b_proj, wout[1]), (gate, gate_b, wgate)):
                sp.dma_start(dst[0:FC], src).then_inc(s_wlater, 16)
                sp.dma_start(dst[FC:FC + 1, NC_ - 1, :], bias).then_inc(s_wlater, 16)
            sp.dma_start(wqkv2[:], w_qkv2).then_inc(s_wlater, 16)
            sp.wait_ge(s_zero_tile, 1)
            for e in range(E + 1):
                last = min((e + 1) * CAP, E * CAP + P)
                sp.dma_start(rows_in[e * CAP:last].rearrange("(r p) d -> p r d", p=P),
                             empty[:].unsqueeze(1).broadcast_to([P, (last - e * CAP) // P, RW])
                             ).then_inc(s_zeroed, 16)
            sp.dma_start(acc[T:T + P], empty[:, 0:D]).then_inc(s_acc, 16)
            with sp.Fori(1, G) as g:
                for t in range(TG):
                    sp.wait_ge(S["tok"], nth("tok", t, g - 1))
                    if t == 0:
                        for u, half in enumerate(halves):
                            sp.dma_start(xin[:, 0, half], x[g * TG][:, half]).then_inc((s_x[0], s_x_rest)[u], 16)
                    else:
                        load_x(t, g * TG + t)
            sp.dma_start(b2s[:], b2.partition_broadcast(P)).then_inc(s_wmoe, 16)
            for e in range(E):
                sp.dma_start(w1s[0:FC, e], w1[:, e]).then_inc(s_wmoe, 16)
                sp.dma_start(w1s[FC:FC + 1, e, NC_ - 1, :], b1[e:e + 1]).then_inc(s_wmoe, 16)
                sp.dma_start(w2s[:, e], w2[:, e]).then_inc(s_wmoe, 16)

            sp.wait_ge(s_xr, TG + NT)
            sp.dma_start(acc[0:T].rearrange("(n p) d -> p n d", p=P), xr[:]).then_inc(s_acc, 16)

            sp.wait_ge(s_tab, 1)
            sp.wait_ge(s_scat, 32 * NT)

            def load_rows(i, b):
                first = sp.value_load(tab_row[0:1, bass.ds(i, 1)], min_val=0, max_val=E * CAP)
                sp.dma_start(xg[:, b], rows_in[bass.ds(first, P)]).then_inc(s_xg[b], 16)

            for b in range(XB):
                load_rows(b, b)
            with sp.Fori(1, BLOCKS // XB) as j:
                for b in range(XB):
                    sp.wait_ge(s_tok_g, XB * j + (b + 1 - XB))
                    load_rows(XB * j + b, b)
            for i in range(BLOCKS // XB * XB, BLOCKS):
                sp.wait_ge(s_tok_g, i + 1 - XB)
                load_rows(i, i % XB)

            sp.wait_ge(s_add, 16 * BLOCKS)
            for u in range(0, LQ, 2):
                sp.dma_start(part(fs, u), part_rows(acc, u)).then_inc(s_fs[u], 16)
            for u in range(LQ):
                sp.wait_ge(s_fin_a, u + 1)
                if u == LQ - 1:
                    sp.wait_ge(s_fin, 1)
                sp.dma_start(part_rows(out, u), part(fo, u)).then_inc(s_out, 16)
            sp.wait_ge(s_out, 16 * LQ)

        @block.gpsimd
        def _(pool):
            nc.gpsimd.memset(minus_half[:], -0.5).then_inc(s_pool_setup, 1)
            nc.gpsimd.memset(big2[:], 0.0).then_inc(s_pool_setup, 1)
            pool.wait_ge(s_pool_setup, 2)
            for h in range(HK):
                nc.gpsimd.memset(vbd[QT * h:QT * h + QT].rearrange("p t q c n -> p (t q c) n")[:, :, VW * h + HD], 1.0
                                 ).then_inc(s_vbd, 1)
            pool.wait_ge(s_vbd, HK)
            nc.gpsimd.tensor_tensor(tick[:], minus_half[:, 0:1], minus_half[:, 0:1], ALU.add).then_inc(s_left, 1)
            pool.wait_ge(s_left, 1)
            nc.gpsimd.tensor_tensor(tick[:], minus_half[:, 0:1], minus_half[:, 0:1], ALU.add).then_inc(s_xr, TG)

            def power(ready, count, done, v, r):
                pool.wait_ge(ready, count)
                nc.gpsimd.tensor_tensor(r, v, minus_half[:, 0:v.shape[1]], ALU.pow).then_inc(done, 1)

            def x1(t, g, steps):
                pool.wait_ge(S["rstd"], nth("proj0", t, g))
                steps.done(nc.gpsimd.tensor_tensor(tick[:], minus_half[:, 0:1], minus_half[:, 0:1], ALU.add))
                steps.join()
                nc.gpsimd.tensor_scalar(hs[:, t], rs[:, t], mv[:, t, 0:1], rstd[:, t, 0:1], ALU.subtract, ALU.mult
                                        ).then_inc(S["x1_there"], 1)

            def x1_x2(t, g):
                pool.wait_ge(S["rstd"], nth("proj1", t, g))
                nc.gpsimd.tensor_tensor(xr[:, bass.ds(g * TG + t, 1)].rearrange("p o d -> p (o d)"), rs[:, t], hs[:, t],
                                        ALU.add).then_inc(s_xr, 1)

            def dispatch(t, g, steps):
                pool.wait_ge(s_zeroed, 16 * (E + 1))
                pool.wait_ge(S["slot"], nth("rank", t, g))
                steps.done(nc.gpsimd.tensor_tensor(slot_g[:, t - 1:t + 1], slot_v[:, t - 1:t + 1],
                                                   empty[:, 0:4].bitcast(I32).rearrange("p (t k) -> p t k", k=2), ALU.add))
                steps.join()
                for u in (t - 1, t):
                    for k in range(2):
                        nc.gpsimd.indirect_dma_start(
                            out=rows_in, out_offset=bass.IndirectOffsetOnAxis(ap=slot_g[:, u, k:k + 1], axis=0),
                            in_=xd[:, u], in_offset=None).then_inc(s_scat, 16)

            with pool.Fori(0, G) as g:
                steps = Steps(pool, s_pool)
                for stage, t in ORDER:
                    if stage == "proj0":
                        power(S["var"], nth("proj0", t, g), S["rstd"], ve[:, t], rstd[:, t])
                    if stage == "proj1":
                        power(S["var"], nth("proj1", t, g), S["rstd"], ve[:, t, 0:1], rstd[:, t, 0:1])
                    if stage == "norm0":
                        x1(t, g, steps)
                    if stage == "norm1":
                        x1_x2(t, g)
                    if stage == "rank":
                        dispatch(t, g, steps)
                pool.sem_clear(s_pool)
                pool.wait_ge(s_scat, (g + 1) * 32 * TG)
                nc.gpsimd.tensor_tensor(tick[:], minus_half[:, 0:1], minus_half[:, 0:1], ALU.add).then_inc(s_left, 1)

            def add_rows(i, b, xb, k, first=False):
                pool.wait_ge(s_y, i + 1)
                if not first:
                    pool.wait_ge(s_add, 16 * i)
                nc.gpsimd.tensor_tensor(tok_g[:, b], xg[:, xb, RW - 1:RW].bitcast(I32), empty[:, 0:1].bitcast(I32),
                                        ALU.add).then_inc(s_tok_g, 1)
                pool.wait_ge(s_tok_g, i + 1)
                nc.gpsimd.tensor_tensor(tick[:], minus_half[:, 0:1], minus_half[:, 0:1], ALU.add).then_inc(s_pool, 1)
                pool.wait_ge(s_pool, k)
                nc.gpsimd.indirect_dma_start(
                    out=acc, out_offset=bass.IndirectOffsetOnAxis(ap=tok_g[:, b], axis=0),
                    in_=yb[:, b], in_offset=None, compute_op=ALU.add).then_inc(s_add, 16)

            pool.wait_ge(s_acc, 16 * 2)
            add_rows(0, 0, 0, 1, first=True)
            for i in range(1, XB):
                add_rows(i, i % 2, i, i + 1)
            pool.sem_clear(s_pool)
            with pool.Fori(1, BLOCKS // XB) as j:
                for b in range(XB):
                    add_rows(XB * j + b, b % 2, b, b + 1)
                pool.sem_clear(s_pool)
            for i in range(BLOCKS // XB * XB, BLOCKS):
                add_rows(i, i % 2, i % XB, i % XB + 1)
            for u in range(LQ):
                power(s_fvar, u + 1, s_frs, part(fve, u), part(frs, u))

        @block.scalar
        def _(act):
            act.dma_start(msk[:], masks).then_inc(s_masks, 16)
            act.dma_start(wheads[:], w_qkv1).then_inc(s_wheads, 16)
            act.dma_start(wqkv1[FC:FC + 1], b_qkv1).then_inc(s_wq1, 16)

            def take_h(t, g):
                act.wait_ge(S["tok"], nth("tok", t, g))
                act.wait_ge(s_xr, xr_before(t, g))
                nc.scalar.activation(hs[:, t], bank(t)[:, 0:D], ACT.Copy).then_inc(S["h"], 1)

            def take_turned(t, g):
                act.wait_ge(S["hT"], nth("turn", t, g))
                nc.scalar.activation(lnT[0:FC, :, t], chunks_of(bank(t, True)), ACT.Copy).then_inc(S["lnT"], 1)

            def chunks_of(b):
                return b[0:FC, 0:NC_ * P].rearrange("p (c q) -> p c q", c=NC_)

            def take_qk(a, t, g):
                n = nth(f"qk{a}", t, g)
                if a == 0:
                    act.wait_ge(s_const, 16)
                act.wait_ge(S["k_mm"], n)
                nc.scalar.activation(kT[:, :, tokens(t)], chunks_of(bank(t)), ACT.Copy).then_inc(S["k_ev"], 1)
                for h in range(HC - ACT_HEADS, HC):
                    nc.scalar.activation(kbd[:, :, h, tokens(t)], chunks_of(bank(t)), ACT.Copy, scale=hmask[0:FC, h:h + 1])
                act.wait_ge(S["q_mm"], n)
                nc.scalar.activation(qT[:, :, tokens(t)], chunks_of(bank(t, True)), ACT.Copy).then_inc(S["q_ev"], 1)

            def take_v(a, t, g):
                act.wait_ge(s_vbd, HK)
                act.wait_ge(S["v_mm"], nth(f"v{a}", t, g))
                for q in range(ACT_QUADS):
                    for h in range(HK):
                        ins = nc.scalar.activation(vbd_part(t, q, h), v_part(t, q, h), ACT.Copy)
                ins.then_inc(S["v_act"], 1)

            def exponentials(a, t, g):
                act.wait_ge(S["scaled"], nth(f"s{a}", t, g))
                nc.scalar.activation(sc[:, t], sc[:, t], ACT.Exp, scale=[D ** -0.5, HD ** -0.5][a]).then_inc(S["prob"], 1)

            def take_pt(a, t, g):
                act.wait_ge(S["pt_mm"], nth(f"pt{a}", t, g))
                nc.scalar.activation(pT[:, t].rearrange("p c q -> p (c q)"), bank(t, True)[:, 0:KC * P], ACT.Copy
                                     ).then_inc(S["pt_ev"], 1)

            def take_at(a, t, g):
                act.wait_ge(S["at_mm"], nth(f"at{a}", t, g))
                nc.scalar.activation(aT[0:FC, t], chunks_of(bank(t, True)), ACT.Copy).then_inc(S["at_ev"], 1)

            def take_ln(a, t, g):
                act.wait_ge(s_ln_gb, 16)
                act.wait_ge(S["ln_mm"], nth(f"ln{a}", t, g))
                for c in range(NC_):
                    ins = nc.scalar.activation(lnT[0:FC, c, t], bank(t, True)[0:FC, c * P:(c + 1) * P], ACT.Identity,
                                               scale=col[:, 2 * a, c:c + 1], bias=col[:, 2 * a + 1, c:c + 1])
                ins.then_inc(S["ln_ev"], 1)

            def second_best(t, g):
                act.wait_ge(S["dif"], nth("gate", t, g))
                nc.scalar.activation(exd[:, t - 1:t + 1], dif[:, t - 1:t + 1], ACT.Exp).then_inc(S["exd"], 1)

            stages = {"tok": take_h, "turn": take_turned, "gate": second_best}
            att_stages = {"qk": take_qk, "v": take_v, "s": exponentials, "pt": take_pt, "at": take_at, "ln": take_ln}
            with act.Fori(0, G) as g:
                for stage, t in ORDER:
                    if stage in stages:
                        stages[stage](t, g)
                    elif stage[:-1] in att_stages:
                        att_stages[stage[:-1]](int(stage[-1]), t, g)

            def turn(i, b):
                act.wait_ge(s_xgfree, i + 1)
                for c in range(NC_):
                    ins = nc.scalar.activation(xgT[0:FC, b, c], ps[0:FC, b, c * P:(c + 1) * P], ACT.Identity,
                                               scale=col[:, 2, c:c + 1], bias=col[:, 3, c:c + 1])
                ins.then_inc(s_xgT, 1)

            def gelu(i, b):
                act.wait_ge(s_up, i + 1)
                for u in range(2):
                    ins = nc.scalar.activation(hid[:, b, u * 3:u * 3 + 3].rearrange("p m q -> p (m q)"),
                                               ps[:, 2 + 2 * b + u, 0:3 * P], ACT.Gelu)
                ins.then_inc(s_hid, 1)

            nc.scalar.activation(warm_act[:], minus_half[:, 0:1], ACT.Gelu)
            turn(0, 0)
            turn(1, 1)
            gelu(0, 0)
            with act.Fori(0, (BLOCKS - 3) // 2) as j:
                for k in range(2):
                    gelu(2 * j + (k + 1), 1 - k)
                    turn(2 * j + (k + 2), k)
            gelu(BLOCKS - 2, 1)
            turn(BLOCKS - 1, 0)
            gelu(BLOCKS - 1, 0)
            act.wait_ge(s_add, 16 * BLOCKS)
            for u in range(1, LQ, 2):
                act.dma_start(part(fs, u), part_rows(acc, u)).then_inc(s_fs[u], 16)
            for n in range(NT):
                if n % HN == 0:
                    act.wait_ge(s_off, n // HN + 1)
                if n != NT - HN:
                    ins = nc.scalar.activation(fo[:, n], fs[:, n], ACT.Identity, scale=frs[:, n:n + 1], bias=off[:, n:n + 1])
                if n % HN == HN - 1:
                    ins.then_inc(s_fin_a, 1)

        @block.vector
        def _(dve):
            s0 = Steps(dve, s_dve_setup)
            nc.vector.memset(ones[:], 1.0).then_inc(s_ones, 1)
            s0.done(nc.vector.memset(empty[:], 0.0))
            nc.vector.memset(run[:], 0.0).then_inc(s_run, 1)
            s0.done(nc.vector.memset(lnT[FC:FC + 1], 1.0))
            s0.done(nc.vector.memset(aT[FC:FC + 1], 1.0))
            s0.done(nc.vector.memset(mask_q[:], 0.0))
            s0.done(nc.vector.memset(mask_k[:], 0.0))
            dve.wait_ge(s_const, 16)
            s0.join()
            nc.vector.tensor_copy(empty[:, RW - 1:RW].bitcast(I32), cst[:, C_TOK + TG:C_END]).then_inc(s_zero_tile, 1)
            s0.done(nc.vector.tensor_copy(toks[:], cst[:, C_TOK:C_TOK + TG]))
            s0.done(nc.vector.tensor_copy(upper[:], cst[:, C_U:C_U + P]))
            dve.wait_ge(s_masks, 16)
            s0.done(nc.vector.tensor_copy(mask_q[0:2], msk[:, 0:P]))
            s0.done(nc.vector.tensor_copy(mask_k[0:2], msk[:, P:]))
            s0.done(nc.vector.tensor_scalar(base[:], cst[:, C_IO:C_IO + E], float(CAP), None, ALU.mult))
            s0.join()
            s0.done(nc.vector.tensor_copy(pos[:, 0], base[:]))
            s0.join()
            nc.vector.tensor_copy(pos[:, 0], base[:]).then_inc(s_counted, TG // 2)
            dve.wait_ge(s_counted, TG // 2)
            dve.wait_ge(s_vbd, HK)
            nc.vector.tensor_copy(pos[:, 0], base[:]).then_inc(s_prep, 1)

            dve.wait_ge(s_wheads, 16)
            nc.vector.tensor_tensor(wqkv1[0:FC].rearrange("p c k (h e) -> p (c k) h e", h=HC),
                                    wheads[:].rearrange("p c k e -> p (c k) e").unsqueeze(2).broadcast_to([FC, NC_ * 3, HC, HD]),
                                    hmask[0:FC].unsqueeze(1).unsqueeze(3).broadcast_to([FC, NC_ * 3, HC, HD]),
                                    ALU.mult).then_inc(s_wq1, 1)

            def keys(a, t, g, s):
                dve.wait_ge(S["k_ev"], nth(f"qk{a}", t, g))
                for h in range(HC - ACT_HEADS):
                    ins = nc.vector.tensor_scalar(kbd[:, :, h, tokens(t)], kT[:, :, tokens(t)], hmask[0:FC, h:h + 1],
                                                  None, ALU.mult)
                ins.then_inc(S["kbd"], 1)

            def values(a, t, g, s):
                dve.wait_ge(S["v_mm"], nth(f"v{a}", t, g))
                for q in range(ACT_QUADS, 4):
                    for h in range(HK):
                        ins = nc.vector.tensor_copy(vbd_part(t, q, h), v_part(t, q, h))
                ins.then_inc(S["v_dve"], 1)

            def maxima(a, t, g, s):
                score = bank(t)[:, 0:H * QT].rearrange("p (h k) -> p h k", h=H)
                dve.wait_ge(S["score"], nth(f"s{a}", t, g))
                s.done(nc.vector.tensor_reduce(mx[:, t], score, AX_X, ALU.max))
                s.join()
                nc.vector.tensor_tensor(sc[:, t], score, mx[:, t].unsqueeze(2).broadcast_to([P, H, QT]),
                                        ALU.subtract).then_inc(S["scaled"], 1)

            def normalised(a, t, g, s):
                heads = bank(t)[:, 0:H * VW].rearrange("p (h d) -> p h d", h=H)
                dve.wait_ge(S["av"], nth(f"av{a}", t, g))
                s.done(nc.vector.reciprocal(ri[:, t], heads[:, :, HD]))
                if a == 1:
                    dve.wait_ge(S["x1_there"], nth("norm0", t, g, both=False))
                s.join()
                nc.vector.tensor_tensor(at[:, t].rearrange("p (h d) -> p h d", h=H), heads[:, :, 0:HD],
                                        ri[:, t].unsqueeze(2).broadcast_to([P, H, HD]), ALU.mult).then_inc(S["at"], 1)

            def residual(a, t, g, s):
                dve.wait_ge(S["proj"], nth(f"proj{a}", t, g))
                s.done(nc.vector.tensor_tensor(rs[:, t], bank(t)[:, 0:D], hs[:, t], ALU.add))
                s.join()
                s.done(nc.vector.bn_stats(st[:, t], rs[:, t]))
                s.join()
                s.done(nc.vector.bn_aggr(mv[:, t], st[:, t]))
                s.join()
                if a == 0:
                    s.done(nc.vector.tensor_scalar(ve[:, t, 1:2], mv[:, t, 1:2], 1.0 + EPS, EPS * EPS, ALU.mult, ALU.add))
                nc.vector.tensor_scalar(ve[:, t, 0:1], mv[:, t, 1:2], EPS, None, ALU.add).then_inc(S["var"], 1)

            def normalise(a, t, g, s):
                if a == 0:
                    dve.wait_ge(S["rstd"], nth("proj0", t, g))
                    nc.vector.tensor_scalar(xh[:, t], rs[:, t], mv[:, t, 0:1], rstd[:, t, 1:2], ALU.subtract, ALU.mult
                                            ).then_inc(S["res"], 1)
                else:
                    dve.wait_ge(s_left, g + 1)
                    dve.wait_ge(S["rstd"], nth("proj1", t, g))
                    nc.vector.tensor_scalar(xd[:, t, 0:D], rs[:, t], mv[:, t, 0:1], rstd[:, t, 0:1], ALU.subtract, ALU.mult
                                            ).then_inc(S["res"], 1)

            def choose(t, g, s):
                tt = slice(t - 1, t + 1)
                dve.wait_ge(S["gate"], nth("gate", t, g))
                s.done(nc.vector.tensor_copy(lg[:, tt], ps[:, t - 1:t + 1, 0:E]))
                s.join()
                for u in (t - 1, t):
                    s.done(nc.vector.max(top[:, u], lg[:, u]))
                s.join()
                for u in (t - 1, t):
                    s.done(nc.vector.max_index(tix[:, u], top[:, u], lg[:, u]))
                nc.vector.tensor_tensor(dif[:, tt], top[:, tt, 1:2], top[:, tt, 0:1], ALU.subtract).then_inc(S["dif"], 1)
                s.join()
                experts = cst[:, C_IO:C_IO + E].unsqueeze(1).unsqueeze(1)
                s.done(nc.vector.tensor_tensor(hot[:, tt], experts.broadcast_to([P, 2, 2, E]),
                                               tix[:, tt, 0:2].unsqueeze(3).broadcast_to([P, 2, 2, E]), ALU.is_equal))
                s.join()
                nc.vector.tensor_tensor(hotb[:, tt], hot[:, tt, 0], hot[:, tt, 1], ALU.add).then_inc(S["hot"], 1)

            def place(t, g, s):
                n, tt = nth("rank", t, g), slice(t - 1, t + 1)
                dve.wait_ge(S["exd"], nth("gate", t, g))
                s.done(nc.vector.tensor_scalar(den[:, tt], exd[:, tt], 1.0, None, ALU.add))
                s.join()
                s.done(nc.vector.reciprocal(w01[:, tt, 0:1], den[:, tt]))
                s.join()
                s.done(nc.vector.tensor_tensor(w01[:, tt, 1:2], w01[:, tt, 0:1], exd[:, tt], ALU.mult))
                s.done(nc.vector.tensor_copy(xd[:, tt, RW - 1:RW].bitcast(I32), toks[:, tt].unsqueeze(2)))
                s.join()
                s.done(nc.vector.tensor_tensor(hw[:, tt], hot[:, tt], w01[:, tt].unsqueeze(3).broadcast_to([P, 2, 2, E]),
                                               ALU.mult))
                s.done(nc.vector.tensor_scalar(toks[:, tt], toks[:, tt], float(TG * P), None, ALU.add))
                dve.wait_ge(S["rank"], n)
                s.done(nc.vector.tensor_tensor(run[:], run[:], hotb[:, t - 1], ALU.add))
                nc.vector.tensor_tensor(pos[:, tt], ps[:, TG + t - 1:TG + t + 1, 0:E],
                                        base[:].unsqueeze(1).broadcast_to([P, 2, E]), ALU.add).then_inc(s_counted, 1)
                s.join()
                nc.vector.tensor_tensor(run[:], run[:], hotb[:, t], ALU.add).then_inc(s_run, 1)
                dve.wait_ge(s_counted, n + TG // 2)
                s.done(nc.vector.tensor_tensor(pick[:, tt], hot[:, tt], pos[:, tt].unsqueeze(2).broadcast_to([P, 2, 2, E]),
                                               ALU.mult))
                s.done(nc.vector.tensor_tensor(xd[:, tt, D:D + E], hw[:, tt, 0], hw[:, tt, 1], ALU.add))
                s.join()
                with nc.allow_low_precision(reason="whole numbers below 2^24"):
                    nc.vector.tensor_reduce(slot_v[:, tt], pick[:, tt], AX_X, ALU.add).then_inc(S["slot"], 1)

            stages = {"gate": choose, "rank": place}
            att_stages = {"qk": keys, "v": values, "s": maxima, "av": normalised, "proj": residual, "norm": normalise}
            with dve.Fori(0, G) as g:
                s = Steps(dve, s_dve)
                for stage, t in ORDER:
                    if stage in stages:
                        stages[stage](t, g, s)
                    elif stage[:-1] in att_stages:
                        att_stages[stage[:-1]](int(stage[-1]), t, g, s)
                s.join()
                dve.sem_clear(s_dve)

            s2 = Steps(dve, s_tables)
            io = cst[:, C_IO:C_IO + E]
            iob = cst[:, C_IO:C_IO + BLOCKS]
            dve.wait_ge(s_cnt, 1)
            s2.done(nc.vector.tensor_copy(cnt[:], ps[:, 2, 0:E]))
            s2.done(nc.vector.tensor_scalar(nblk[:], io, float(P), None, ALU.mult))
            s2.join()
            s2.done(nc.vector.tensor_tensor(cmpb[:], cnt[:].unsqueeze(2).broadcast_to([P, E, E]),
                                            nblk[:].unsqueeze(1).broadcast_to([P, E, E]), ALU.is_gt))
            s2.join()
            s2.done(nc.vector.tensor_reduce(nblk[:], cmpb[:], AX_X, ALU.add))
            s2.join()
            s2.done(nc.vector.tensor_copy(lastb[:], nblk[:]))
            for e in range(1, E):
                s2.join()
                s2.done(nc.vector.tensor_tensor(lastb[:, e:e + 1], lastb[:, e - 1:e], lastb[:, e:e + 1], ALU.add))
            s2.join()
            iob_e = iob.unsqueeze(2).broadcast_to([P, BLOCKS, E])
            last_e = lastb[:].unsqueeze(1).broadcast_to([P, BLOCKS, E])
            s2.done(nc.vector.tensor_tensor(cmp2[:], last_e, iob_e, ALU.is_le))
            s2.join()
            s2.done(nc.vector.tensor_reduce(eof[:], cmp2[:], AX_X, ALU.add))
            s2.done(nc.vector.tensor_tensor(cmp3[:], cmp2[:], nblk[:].unsqueeze(1).broadcast_to([P, BLOCKS, E]), ALU.mult))
            s2.join()
            s2.done(nc.vector.tensor_reduce(fst[:], cmp3[:], AX_X, ALU.add))
            s2.done(nc.vector.tensor_scalar(rowf[:], eof[:], float(CAP // P), None, ALU.mult))
            s2.join()
            s2.done(nc.vector.tensor_tensor(fst[:], iob, fst[:], ALU.subtract))
            s2.join()
            s2.done(nc.vector.tensor_tensor(rowf[:], rowf[:], fst[:], ALU.add))
            s2.done(nc.vector.tensor_scalar(tab_e[:], eof[:], float(E - 1), None, ALU.min))
            s2.done(nc.vector.memset(xgT[FC:FC + 1], 1.0))
            s2.join()
            nc.vector.tensor_scalar(tab_row[:], rowf[:], float(P), float(E * CAP), ALU.mult, ALU.min).then_inc(s_tab, 1)
            dve.wait_ge(s_tab, 1)
            dve.wait_ge(s_wmoe, 16 * (1 + 3 * E))

            def expert(i):
                return dve.value_load(tab_e[0:1, bass.ds(i, 1)], min_val=0, max_val=E - 1)

            def stage_w1(i, b):
                e = expert(i)
                nc.vector.tensor_copy(w1c[0:FC, b, 0], w1s[0:FC, bass.ds(e, 1), 0].rearrange("p o n -> p (o n)"))
                nc.vector.tensor_copy(w1c[:, b, 1], w1s[:, bass.ds(e, 1), 1].rearrange("p o n -> p (o n)")
                                      ).then_inc(s_w1c, 1)

            def take_y(i, b, xb, k, first=False):
                e = expert(i)
                dve.wait_ge(s_down, i + 1)
                if not first:
                    dve.wait_ge(s_add, 16 * (i - 1))
                nc.vector.tensor_tensor(yb[:, b], ps[:, 6 + b, 0:D], b2s[:, bass.ds(e, 1)].rearrange("p o n -> p (o n)"),
                                        ALU.add).then_inc(s_y_biased, 1)
                dve.wait_ge(s_y_biased, k)
                nc.vector.tensor_tensor(yb[:, b], yb[:, b], xg[:, xb, bass.ds(e + D, 1)].broadcast_to([P, D]),
                                        ALU.mult).then_inc(s_y, 1)

            stage_w1(0, 0)
            stage_w1(1, 1)
            for i in range(XB):
                dve.wait_ge(s_up, i + 1)
                stage_w1(i + 2, i % 2)
                take_y(i, i % 2, i, i + 1, first=i < 2)
            dve.sem_clear(s_y_biased)
            with dve.Fori(1, BLOCKS // XB) as j:
                for b in range(XB):
                    dve.wait_ge(s_up, XB * j + (b + 1))
                    stage_w1(XB * j + b + 2, b % 2)
                    take_y(XB * j + b, b % 2, b, b + 1)
                dve.sem_clear(s_y_biased)
            for i in range(BLOCKS // XB * XB, BLOCKS):
                if i + 2 < BLOCKS:
                    dve.wait_ge(s_up, i + 1)
                    stage_w1(i + 2, i % 2)
                take_y(i, i % 2, i % XB, i % XB + 1)

            s3 = Steps(dve, s_stats)

            def statistics(u):
                dve.wait_ge(s_fs[u], 16)
                for n in range(u * HN, (u + 1) * HN):
                    s3.done(nc.vector.bn_stats(fst6[:, n], fs[:, n]))
                s3.join()
                for n in range(u * HN, (u + 1) * HN):
                    s3.done(nc.vector.bn_aggr(fmv[:, n], fst6[:, n]))
                s3.join()
                nc.vector.tensor_scalar(part(fve, u), part(fmv, u)[:, :, 1], EPS, None, ALU.add).then_inc(s_fvar, 1)

            def finish(u):
                dve.wait_ge(s_frs, u + 1)
                nc.vector.scalar_tensor_tensor(out=part(off, u), in0=part(fmv, u)[:, :, 0], scalar=-1.0, in1=part(frs, u),
                                               op0=ALU.mult, op1=ALU.mult).then_inc(s_off, 1)

            statistics(0)
            for u in range(1, LQ):
                statistics(u)
                finish(u - 1)
            finish(LQ - 1)
            n = NT - HN
            nc.vector.tensor_scalar(fo[:, n], fs[:, n], fmv[:, n, 0:1], frs[:, n:n + 1], ALU.subtract, ALU.mult
                                    ).then_inc(s_fin, 1)

        @block.tensor
        def _(pe):
            mm = nc.tensor.matmul
            tr = nc.tensor.transpose

            def keep_warm(n):
                for i in range(n):
                    mm(bank(0, True)[:, 0:P], ones[:], ones[:], start=True, stop=True)

            pe.wait_ge(s_ones, 1)
            keep_warm(32)
            pe.wait_ge(s_wtok, 16)

            def embed(t, g):
                pe.wait_ge(s_x[t], (g + 1) * 16)
                for k in range(KIN):
                    if t == 0 and k == KIN // 2:
                        pe.wait_ge(s_x_rest, (g + 1) * 16)
                        pe.wait_ge(s_wtok_rest, 16)
                    ins = mm(bank(t)[:, 0:D], xin[:, t, k], wtok[:, k], start=(k == 0), stop=(k == KIN - 1))
                ins.then_inc(S["tok"], 1)

            def turn_tile(t, src):
                for c in range(NC_):
                    ins = tr(bank(t, True)[0:FC, c * P:(c + 1) * P], src[:, t, c * FC:(c + 1) * FC], ident)
                return ins

            def turn_h(t, g):
                if t == 0:
                    pe.wait_ge(s_prep, 1)
                pe.wait_ge(S["h"], nth("tok", t, g))
                pe.wait_ge(s_counted, nth("rank", t | 1, g))
                turn_tile(t, hs).then_inc(S["hT"], 1)

            def keys_queries(a, t, g):
                if a == 0:
                    pe.wait_ge(s_wq1, 16 + 1)
                    pe.wait_ge(S["lnT"], nth("turn", t, g))
                else:
                    pe.wait_ge(S["ln_ev"], nth("ln0", t, g))
                for second, kind, name in ((False, 1, "k_mm"), (True, 0, "q_mm")):
                    for c in range(NC_):
                        dst = bank(t, second)[0:FC, c * P:(c + 1) * P]
                        if a == 0:
                            ins = mm(dst, wqkv1[:, c, kind], lnT[:, c, t], start=True, stop=True)
                        else:
                            for k in range(NC_):
                                ins = mm(dst, wqkv2[:, k, kind * D + c * FC:kind * D + (c + 1) * FC], lnT[0:FC, k, t],
                                         start=(k == 0), stop=(k == NC_ - 1))
                    ins.then_inc(S[name], 1)

            def values(a, t, g):
                pe.wait_ge(S["q_ev"], nth(f"qk{a}", t, g))
                for c in range(NC_):
                    if a == 0:
                        ins = mm(bank(t, True)[:, c * FC:(c + 1) * FC], lnT[:, c, t], wqkv1[:, c, 2], start=True, stop=True)
                    else:
                        ins = mm(bank(t, True)[:, 0:D], lnT[0:FC, c, t], wqkv2[:, c, 2 * D:3 * D],
                                 start=(c == 0), stop=(c == NC_ - 1))
                ins.then_inc(S["v_mm"], 1)

            def scores(a, t, g):
                pe.wait_ge(S["kbd"], nth(f"qk{a}", t, g))
                mm(bank(t)[:, 0:H * QT], mask_q[:], mask_k[:], start=True, stop=False, skip_group_check=True)
                for c in range(NC_):
                    for q in range(4):
                        tok = slice(t * P + q * QT, t * P + (q + 1) * QT)
                        ins = mm(bank(t)[q * QT:(q + 1) * QT, c * HC * QT:(c + 1) * HC * QT], qT[:, c, tok],
                                 kbd[:, c, :, tok], start=False, stop=(c == NC_ - 1), skip_group_check=True)
                ins.then_inc(S["score"], 1)

            def turn_probs(a, t, g):
                pe.wait_ge(S["v_act"], nth(f"v{a}", t, g))
                pe.wait_ge(S["v_dve"], nth(f"v{a}", t, g))
                pe.wait_ge(S["prob"], nth(f"s{a}", t, g))
                for c in range(KC):
                    ins = tr(bank(t, True)[:, c * P:(c + 1) * P],
                             sc[:, t].rearrange("p h k -> p (h k)")[:, c * P:(c + 1) * P], ident)
                ins.then_inc(S["pt_mm"], 1)

            def attend(a, t, g):
                pe.wait_ge(S["pt_ev"], nth(f"pt{a}", t, g))
                for c in range(KC):
                    for q in range(4):
                        ins = mm(bank(t)[q * QT:(q + 1) * QT, c * HK * VW:(c + 1) * HK * VW],
                                 pT[:, t, c, q * QT:(q + 1) * QT], vbd[:, t, q, c], start=True, stop=True)
                ins.then_inc(S["av"], 1)

            def turn_attended(a, t, g):
                pe.wait_ge(S["at"], nth(f"av{a}", t, g))
                turn_tile(t, at).then_inc(S["at_mm"], 1)

            def project(a, t, g):
                pe.wait_ge(s_wlater, 16 * 7)
                pe.wait_ge(S["at_ev"], nth(f"at{a}", t, g))
                for c in range(NC_):
                    K = FC + (c == NC_ - 1)
                    ins = mm(bank(t)[:, 0:D], aT[0:K, t, c], wout[a][0:K, c], start=(c == 0), stop=(c == NC_ - 1))
                ins.then_inc(S["proj"], 1)

            def turn_ln(a, t, g):
                pe.wait_ge(S["res"], nth(f"norm{a}", t, g))
                turn_tile(t, (xh, xd)[a]).then_inc(S["ln_mm"], 1)

            def gates(t, g):
                pe.wait_ge(S["ln_ev"], nth("ln1", later("ln1", t), g))
                for u in (t - 1, t):
                    for c in range(NC_):
                        K = FC + (c == NC_ - 1)
                        ins = mm(bank(u)[:, 0:E], lnT[0:K, c, u], wgate[0:K, c], start=(c == 0), stop=(c == NC_ - 1))
                ins.then_inc(S["gate"], 1)

            def count(t, g):
                pe.wait_ge(S["hot"], nth("gate", t, g))
                pe.wait_ge(s_run, nth("rank", t, g))
                for u in (t - 1, t):
                    dst = bank(u, True)[:, 0:E]
                    mm(dst, upper[:], hotb[:, u], start=True, stop=False)
                    if u == t:
                        mm(dst, ones[:], hotb[:, t - 1], start=False, stop=False)
                    ins = mm(dst, ones[:], run[:], start=False, stop=True)
                ins.then_inc(S["rank"], 1)

            stages = {"tok": embed, "turn": turn_h, "gate": gates, "rank": count}
            att_stages = {"qk": keys_queries, "v": values, "s": scores, "pt": turn_probs, "av": attend,
                          "at": turn_attended, "proj": project, "ln": turn_ln}
            with pe.Fori(0, G) as g:
                for stage, t in ORDER:
                    if stage in stages:
                        stages[stage](t, g)
                    elif stage[:-1] in att_stages:
                        att_stages[stage[:-1]](int(stage[-1]), t, g)
            pe.wait_ge(s_run, NT // 2 + 1)
            mm(ps[:, 2, 0:E], ones[:], run[:], start=True, stop=True).then_inc(s_cnt, 1)

            pe.wait_ge(s_tab, 1)
            pe.wait_ge(s_wmoe, 16 * (1 + 3 * E))
            keep_warm(32)

            def turn_rows(b, xb, j):
                pe.wait_ge(s_xg[xb], 16 * (j + 1))
                for c in range(NC_):
                    ins = tr(ps[0:FC, b, c * P:(c + 1) * P], xg[:, xb, c * FC:(c + 1) * FC], ident)
                ins.then_inc(s_xgfree, 1)

            def up(i, b):
                pe.wait_ge(s_w1c, i + 1)
                pe.wait_ge(s_xgT, i + 1)
                for m in range(MH):
                    for c in range(NC_):
                        K = FC + (c == NC_ - 1)
                        ins = mm(ps[:, 2 + 2 * b + m // 3, m % 3 * P:(m % 3 + 1) * P], w1c[0:K, b, c, m * P:(m + 1) * P],
                                 xgT[0:K, b, c], start=(c == 0), stop=(c == NC_ - 1))
                ins.then_inc(s_up, 1)

            def down(i, b):
                e = pe.value_load(tab_e[0:1, bass.ds(i, 1)], min_val=0, max_val=E - 1)
                pe.wait_ge(s_hid, i + 1)
                for m in range(MH):
                    ins = mm(ps[:, 6 + b, 0:D], hid[:, b, m], w2s[:, bass.ds(e, 1), m].rearrange("p o n -> p (o n)"),
                             start=(m == 0), stop=(m == MH - 1))
                ins.then_inc(s_down, 1)

            turn_rows(0, 0, 0)
            turn_rows(1, 1, 0)
            up(0, 0)
            with pe.Fori(0, (BLOCKS - 3) // XB) as j:
                for b in range(XB):
                    i = XB * j + b
                    up(i + 1, 1 - b % 2)
                    turn_rows(b % 2, (b + 2) % XB, j + (b + 2) // XB)
                    down(i, b % 2)
            for i in range((BLOCKS - 3) // XB * XB, BLOCKS - 1):
                up(i + 1, (i + 1) % 2)
                if i + 2 < BLOCKS:
                    turn_rows(i % 2, (i + 2) % XB, (i + 2) // XB)
                if i == BLOCKS - 2:
                    pe.wait_ge(s_y, BLOCKS - 3)
                down(i, i % 2)
            pe.wait_ge(s_y, BLOCKS - 2)
            down(BLOCKS - 1, 0)


def kernel(x, L0_tok_W, L0_attn_W_qkv, L0_attn_b_qkv, L0_attn_W_out, L0_attn_b_out, L0_ffn_ln1_g, L0_ffn_ln1_b,
           L0_ffn_qkv_w, L0_ffn_proj_w, L0_ffn_proj_b, L0_ffn_ln2_g, L0_ffn_ln2_b, L0_ffn_gate_w, L0_ffn_gate_b,
           L0_ffn_w1, L0_ffn_b1, L0_ffn_w2, L0_ffn_b2):
    import concourse.bacc as bacc
    from concourse.bass_utils import run_bass_kernel_spmd

    def laid(a):
        return np.ascontiguousarray(a)

    def chunks(w):
        return laid(np.asarray(w).reshape(NC_, FC, -1).transpose(1, 0, 2))

    n_img, side, p = x.shape[0], x.shape[2] // 16, 16
    patches = np.asarray(x).reshape(n_img, 3, side, p, side, p).transpose(0, 2, 4, 3, 5, 1)
    patches = patches.reshape(NT, P, KIN, P).transpose(0, 3, 2, 1)
    b_qkv = np.asarray(L0_attn_b_qkv).reshape(H, 3, HD).transpose(1, 0, 2).reshape(1, 3, NC_, FC).transpose(0, 2, 1, 3)
    lns = [np.asarray(v).reshape(1, NC_, FC) for v in (L0_ffn_ln1_g, L0_ffn_ln1_b, L0_ffn_ln2_g, L0_ffn_ln2_b)]
    arrays = {
        "consts": constants(),
        "masks": image_masks(),
        "patches": laid(patches),
        "w_tok": laid(np.asarray(L0_tok_W).T.reshape(KIN, P, D).transpose(1, 0, 2)),
        "w_qkv1": laid(np.asarray(L0_attn_W_qkv).reshape(NC_, HC * HD, 3, HD).transpose(1, 0, 2, 3)),
        "b_qkv1": laid(b_qkv),
        "ln_gb": laid(np.concatenate(lns).transpose(2, 0, 1)),
        "w_out1": chunks(L0_attn_W_out),
        "b_out1": laid(np.asarray(L0_attn_b_out).reshape(1, D)),
        "w_qkv2": chunks(np.asarray(L0_ffn_qkv_w).T),
        "w_proj": chunks(np.asarray(L0_ffn_proj_w).T),
        "b_proj": laid(np.asarray(L0_ffn_proj_b).reshape(1, D)),
        "gate": chunks(np.asarray(L0_ffn_gate_w).T),
        "gate_b": laid(np.asarray(L0_ffn_gate_b).reshape(1, E)),
        "w1": laid(np.asarray(L0_ffn_w1).transpose(2, 0, 1).reshape(NC_, FC, E, HID).transpose(1, 2, 0, 3)),
        "b1": laid(L0_ffn_b1),
        "w2": laid(np.asarray(L0_ffn_w2).transpose(2, 0, 1).reshape(MH, P, E, D).transpose(1, 2, 0, 3)),
        "b2": laid(L0_ffn_b2),
    }
    nc = bacc.Bacc("TRN2", target_bir_lowering=False, num_devices=1)
    args = [nc.dram_tensor(k, a.shape, mybir.dt.from_np(a.dtype), kind="ExternalInput").ap() for k, a in arrays.items()]
    out = nc.dram_tensor("out", (T, D), F32, kind="ExternalOutput").ap()
    vit_block(nc, *args, out)
    got = run_bass_kernel_spmd(nc, [arrays], core_ids=[0]).results[0]["out"]
    return got.reshape(n_img, side * side, D)
```
